# Optimizing a Trainium2 kernel written in Bass

```python
import numpy as np
import jax
import jax.numpy as jnp

def _softmax(x, axis=-1):
    return jax.nn.softmax(x, axis=axis)

def _gelu(x):
    return jax.nn.gelu(x, approximate=True)

def _silu(x):
    return jax.nn.silu(x)

def _sigmoid(x):
    return jax.nn.sigmoid(x)

def _layernorm(x, axis=-1, eps=1e-05):
    m = jnp.mean(x, axis=axis, keepdims=True)
    v = jnp.var(x, axis=axis, keepdims=True)
    return (x - m) / jnp.sqrt(v + eps)

def _scatter_add(tgt, idx, src, axis=0):
    return tgt.at[idx].add(src)

def _segment_sum(src, seg, n):
    return jax.ops.segment_sum(src, seg, n)
kernel_name = 'mk_audio_tower_d1_tok_audfeat512_r4_e449c4'

def setup_inputs(seed: int=0):
    np.random.seed(seed)
    _w = jnp.asarray

    def _rec_inputs():
        import jax
        import jax.numpy as jnp
        _rk = jax.random.key(seed)
        x = -0.000154849 + 1.00019 * jax.random.normal(jax.random.fold_in(_rk, 1), (128, 125, 40), jnp.float32)
        return x
    x = _rec_inputs()

    def _L0_tok_setup():
        import jax, jax.numpy as jnp
        import numpy as np
        CTX = 5
        DIL = 1
        EPS = 1e-05
        key = jax.random.key(seed)
        k1, k2, k3 = jax.random.split(key, 3)
        B, T, D, O = (32, 1024, 40, 128)
        x = jax.random.normal(k1, (B, T, D), dtype=jnp.float32)
        W = jax.random.normal(k2, (O, D * CTX), dtype=jnp.float32) / np.sqrt(D * CTX)
        b = jax.random.normal(k3, (O,), dtype=jnp.float32) * 0.01
        gamma = jnp.ones((O,), dtype=jnp.float32)
        beta = jnp.zeros((O,), dtype=jnp.float32)
        return {'x': x, 'W': W, 'b': b, 'gamma': gamma, 'beta': beta}
    _L0_tok_all = _L0_tok_setup()
    _L0_tok_in = {k: v for k, v in _L0_tok_all.items() if k in ('W', 'b', 'gamma', 'beta')}
    del _L0_tok_all

    def _L0_attn_setup():
        import jax, jax.numpy as jnp
        import numpy as np
        D_MODEL = 128
        N_HEADS = 8
        DH = D_MODEL // N_HEADS
        Q_PROJ = D_MODEL // 2
        KV_PROJ = 2 * D_MODEL // 3
        ROPE_DIM = D_MODEL // 8
        R = ROPE_DIM // N_HEADS
        THETA = 10000.0
        EPS = 1e-05
        B, S = (2, 512)

        def layernorm(x, g, b):
            m = jnp.mean(x, axis=-1, keepdims=True)
            v = jnp.var(x, axis=-1, keepdims=True)
            return (x - m) * jax.lax.rsqrt(v + EPS) * g + b

        def rope_cos_sin(seq_len, dtype):
            inv_freq = THETA ** (-jnp.arange(0, R, 2, dtype=jnp.float32) / R)
            ang = jnp.arange(seq_len, dtype=jnp.float32)[:, None] * inv_freq
            cos = jnp.concatenate([jnp.cos(ang), jnp.cos(ang)], axis=-1)
            sin = jnp.concatenate([jnp.sin(ang), jnp.sin(ang)], axis=-1)
            return (cos.astype(dtype), sin.astype(dtype))

        def apply_rope(x, cos, sin):
            x1, x2 = jnp.split(x, 2, axis=-1)
            rot = jnp.concatenate([-x2, x1], axis=-1)
            return x * cos + rot * sin

        def _reference_tuple_inner(x, W_dq, W_uq, W_qr, W_dkv, W_ukv, W_kr, W_o, q_ln_g, q_ln_b, kv_ln_g, kv_ln_b):
            b, s, d = x.shape
            cq = layernorm(x @ W_dq, q_ln_g, q_ln_b)
            Q = (cq @ W_uq).reshape(b, s, N_HEADS, DH).transpose(0, 2, 1, 3)
            Qr = (cq @ W_qr).reshape(b, s, N_HEADS, R).transpose(0, 2, 1, 3)
            cos, sin = rope_cos_sin(s, x.dtype)
            Qr = apply_rope(Qr, cos, sin)
            q = jnp.concatenate([Q, Qr], axis=-1)
            ckv = layernorm(x @ W_dkv, kv_ln_g, kv_ln_b)
            KV = ckv @ W_ukv
            K, V = (KV[..., :D_MODEL], KV[..., D_MODEL:])
            K = K.reshape(b, s, N_HEADS, DH).transpose(0, 2, 1, 3)
            Kr = (x @ W_kr).reshape(b, s, N_HEADS, R).transpose(0, 2, 1, 3)
            Kr = apply_rope(Kr, cos, sin)
            k = jnp.concatenate([K, Kr], axis=-1)
            v = V.reshape(b, s, N_HEADS, DH).transpose(0, 2, 1, 3)
            scale = 1.0 / jnp.sqrt(jnp.asarray(DH + R, x.dtype))
            scores = jnp.einsum('bhqd,bhkd->bhqk', q, k) * scale
            mask = jnp.tril(jnp.ones((s, s), dtype=bool))
            scores = jnp.where(mask, scores, jnp.finfo(scores.dtype).min)
            attn = jax.nn.softmax(scores, axis=-1)
            out = jnp.einsum('bhqk,bhkd->bhqd', attn, v)
            out = out.transpose(0, 2, 1, 3).reshape(b, s, d)
            return (out @ W_o.T, ckv)
        key = jax.random.key(seed)
        ks = jax.random.split(key, 9)
        p = lambda k, shape: 0.01 * jax.random.normal(k, shape, jnp.float32)
        return {'x': jax.random.normal(ks[0], (B, S, D_MODEL), jnp.float32), 'W_dq': p(ks[1], (D_MODEL, Q_PROJ)), 'W_uq': p(ks[2], (Q_PROJ, D_MODEL)), 'W_qr': p(ks[3], (Q_PROJ, ROPE_DIM)), 'W_dkv': p(ks[4], (D_MODEL, KV_PROJ)), 'W_ukv': p(ks[5], (KV_PROJ, 2 * D_MODEL)), 'W_kr': p(ks[6], (D_MODEL, ROPE_DIM)), 'W_o': p(ks[7], (D_MODEL, D_MODEL)), 'q_ln_g': jnp.ones((Q_PROJ,), jnp.float32), 'q_ln_b': jnp.zeros((Q_PROJ,), jnp.float32), 'kv_ln_g': jnp.ones((KV_PROJ,), jnp.float32), 'kv_ln_b': jnp.zeros((KV_PROJ,), jnp.float32)}
    _L0_attn_all = _L0_attn_setup()
    _L0_attn_in = {k: v for k, v in _L0_attn_all.items() if k in ('W_dq', 'W_uq', 'W_qr', 'W_dkv', 'W_ukv', 'W_kr', 'W_o', 'q_ln_g', 'q_ln_b', 'kv_ln_g', 'kv_ln_b')}
    del _L0_attn_all

    def _L0_ffn_setup():
        import jax, jax.numpy as jnp
        import numpy as np
        B, S, D, F, E, K, H = (4, 256, 128, 512, 8, 2, 8)
        HEAD_DIM = D // H

        def _layernorm(x, g, b):
            m = x.mean(-1, keepdims=True)
            v = ((x - m) ** 2).mean(-1, keepdims=True)
            return (x - m) * jax.lax.rsqrt(v + 1e-05) * g + b

        def _expert(x, Wqkv, bqkv, Wo, bo, g1, be1, W1, bf1, W2, bf2, g2, be2):
            b, s, d = x.shape
            qkv = x @ Wqkv.T + bqkv
            q, k, v = jnp.split(qkv, 3, axis=-1)
            to_heads = lambda t: t.reshape(b, s, H, HEAD_DIM).transpose(0, 2, 1, 3)
            q, k, v = (to_heads(q), to_heads(k), to_heads(v))
            scale = 1.0 / np.sqrt(HEAD_DIM).astype(np.float32)
            attn = jax.nn.softmax(jnp.einsum('bhqd,bhkd->bhqk', q * scale, k), axis=-1)
            ctx = jnp.einsum('bhqk,bhkd->bhqd', attn, v).transpose(0, 2, 1, 3).reshape(b, s, d)
            ctx = ctx @ Wo.T + bo
            x = _layernorm(x + ctx, g1, be1)
            h = jax.nn.gelu(x @ W1.T + bf1, approximate=False)
            h = jax.nn.gelu(h @ W2.T + bf2, approximate=False)
            return _layernorm(x + h, g2, be2)
        key = jax.random.key(seed)
        ks = jax.random.split(key, 8)
        s = 0.02
        return {'x': jax.random.normal(ks[0], (B, S, D), jnp.float32), 'gate_Wk': jax.random.normal(ks[1], (D, D), jnp.float32) * s, 'gate_bk': jnp.zeros((D,), jnp.float32), 'expert_queries': jax.random.normal(ks[2], (E, D), jnp.float32), 'Wqkv': jax.random.normal(ks[3], (E, 3 * D, D), jnp.float32) * s, 'bqkv': jnp.zeros((E, 3 * D), jnp.float32), 'Wo': jax.random.normal(ks[4], (E, D, D), jnp.float32) * s, 'bo': jnp.zeros((E, D), jnp.float32), 'g1': jnp.ones((E, D), jnp.float32), 'be1': jnp.zeros((E, D), jnp.float32), 'W1': jax.random.normal(ks[5], (E, F, D), jnp.float32) * s, 'bf1': jnp.zeros((E, F), jnp.float32), 'W2': jax.random.normal(ks[6], (E, D, F), jnp.float32) * s, 'bf2': jnp.zeros((E, D), jnp.float32), 'g2': jnp.ones((E, D), jnp.float32), 'be2': jnp.zeros((E, D), jnp.float32)}
    _L0_ffn_all = _L0_ffn_setup()
    _L0_ffn_in = {k: v for k, v in _L0_ffn_all.items() if k in ('gate_Wk', 'gate_bk', 'expert_queries', 'Wqkv', 'bqkv', 'Wo', 'bo', 'g1', 'be1', 'W1', 'bf1', 'W2', 'bf2', 'g2', 'be2')}
    del _L0_ffn_all
    return {'x': x, 'L0_tok_W': _L0_tok_in['W'], 'L0_tok_b': _L0_tok_in['b'], 'L0_tok_gamma': _L0_tok_in['gamma'], 'L0_tok_beta': _L0_tok_in['beta'], 'L0_attn_W_dq': _L0_attn_in['W_dq'], 'L0_attn_W_uq': _L0_attn_in['W_uq'], 'L0_attn_W_qr': _L0_attn_in['W_qr'], 'L0_attn_W_dkv': _L0_attn_in['W_dkv'], 'L0_attn_W_ukv': _L0_attn_in['W_ukv'], 'L0_attn_W_kr': _L0_attn_in['W_kr'], 'L0_attn_W_o': _L0_attn_in['W_o'], 'L0_attn_q_ln_g': _L0_attn_in['q_ln_g'], 'L0_attn_q_ln_b': _L0_attn_in['q_ln_b'], 'L0_attn_kv_ln_g': _L0_attn_in['kv_ln_g'], 'L0_attn_kv_ln_b': _L0_attn_in['kv_ln_b'], 'L0_ffn_gate_Wk': _L0_ffn_in['gate_Wk'], 'L0_ffn_gate_bk': _L0_ffn_in['gate_bk'], 'L0_ffn_expert_queries': _L0_ffn_in['expert_queries'], 'L0_ffn_Wqkv': _L0_ffn_in['Wqkv'], 'L0_ffn_bqkv': _L0_ffn_in['bqkv'], 'L0_ffn_Wo': _L0_ffn_in['Wo'], 'L0_ffn_bo': _L0_ffn_in['bo'], 'L0_ffn_g1': _L0_ffn_in['g1'], 'L0_ffn_be1': _L0_ffn_in['be1'], 'L0_ffn_W1': _L0_ffn_in['W1'], 'L0_ffn_bf1': _L0_ffn_in['bf1'], 'L0_ffn_W2': _L0_ffn_in['W2'], 'L0_ffn_bf2': _L0_ffn_in['bf2'], 'L0_ffn_g2': _L0_ffn_in['g2'], 'L0_ffn_be2': _L0_ffn_in['be2']}

def reference(x, L0_tok_W, L0_tok_b, L0_tok_gamma, L0_tok_beta, L0_attn_W_dq, L0_attn_W_uq, L0_attn_W_qr, L0_attn_W_dkv, L0_attn_W_ukv, L0_attn_W_kr, L0_attn_W_o, L0_attn_q_ln_g, L0_attn_q_ln_b, L0_attn_kv_ln_g, L0_attn_kv_ln_b, L0_ffn_gate_Wk, L0_ffn_gate_bk, L0_ffn_expert_queries, L0_ffn_Wqkv, L0_ffn_bqkv, L0_ffn_Wo, L0_ffn_bo, L0_ffn_g1, L0_ffn_be1, L0_ffn_W1, L0_ffn_bf1, L0_ffn_W2, L0_ffn_bf2, L0_ffn_g2, L0_ffn_be2):
    import jax
    import jax.numpy as jnp

    def _L0_tok_ref(x, W, b, gamma, beta):
        import jax, jax.numpy as jnp
        import numpy as np
        CTX = 5
        DIL = 1
        EPS = 1e-05
        B, T, D = x.shape
        newT = T - (CTX - 1) * DIL
        windows = jnp.concatenate([x[:, i * DIL:i * DIL + newT, :] for i in range(CTX)], axis=-1)
        h = jax.nn.relu(jnp.einsum('btk,ok->bto', windows, W) + b)
        mean = jnp.mean(h, axis=(0, 1))
        var = jnp.mean(jnp.square(h - mean), axis=(0, 1))
        out = (h - mean) * jax.lax.rsqrt(var + EPS) * gamma + beta
        return out

    def _L0_attn_ref(x, W_dq, W_uq, W_qr, W_dkv, W_ukv, W_kr, W_o, q_ln_g, q_ln_b, kv_ln_g, kv_ln_b):
        import jax, jax.numpy as jnp
        import numpy as np
        D_MODEL = 128
        N_HEADS = 8
        DH = D_MODEL // N_HEADS
        Q_PROJ = D_MODEL // 2
        KV_PROJ = 2 * D_MODEL // 3
        ROPE_DIM = D_MODEL // 8
        R = ROPE_DIM // N_HEADS
        THETA = 10000.0
        EPS = 1e-05
        B, S = (2, 512)

        def layernorm(x, g, b):
            m = jnp.mean(x, axis=-1, keepdims=True)
            v = jnp.var(x, axis=-1, keepdims=True)
            return (x - m) * jax.lax.rsqrt(v + EPS) * g + b

        def rope_cos_sin(seq_len, dtype):
            inv_freq = THETA ** (-jnp.arange(0, R, 2, dtype=jnp.float32) / R)
            ang = jnp.arange(seq_len, dtype=jnp.float32)[:, None] * inv_freq
            cos = jnp.concatenate([jnp.cos(ang), jnp.cos(ang)], axis=-1)
            sin = jnp.concatenate([jnp.sin(ang), jnp.sin(ang)], axis=-1)
            return (cos.astype(dtype), sin.astype(dtype))

        def apply_rope(x, cos, sin):
            x1, x2 = jnp.split(x, 2, axis=-1)
            rot = jnp.concatenate([-x2, x1], axis=-1)
            return x * cos + rot * sin

        def _reference_tuple_inner(x, W_dq, W_uq, W_qr, W_dkv, W_ukv, W_kr, W_o, q_ln_g, q_ln_b, kv_ln_g, kv_ln_b):
            b, s, d = x.shape
            cq = layernorm(x @ W_dq, q_ln_g, q_ln_b)
            Q = (cq @ W_uq).reshape(b, s, N_HEADS, DH).transpose(0, 2, 1, 3)
            Qr = (cq @ W_qr).reshape(b, s, N_HEADS, R).transpose(0, 2, 1, 3)
            cos, sin = rope_cos_sin(s, x.dtype)
            Qr = apply_rope(Qr, cos, sin)
            q = jnp.concatenate([Q, Qr], axis=-1)
            ckv = layernorm(x @ W_dkv, kv_ln_g, kv_ln_b)
            KV = ckv @ W_ukv
            K, V = (KV[..., :D_MODEL], KV[..., D_MODEL:])
            K = K.reshape(b, s, N_HEADS, DH).transpose(0, 2, 1, 3)
            Kr = (x @ W_kr).reshape(b, s, N_HEADS, R).transpose(0, 2, 1, 3)
            Kr = apply_rope(Kr, cos, sin)
            k = jnp.concatenate([K, Kr], axis=-1)
            v = V.reshape(b, s, N_HEADS, DH).transpose(0, 2, 1, 3)
            scale = 1.0 / jnp.sqrt(jnp.asarray(DH + R, x.dtype))
            scores = jnp.einsum('bhqd,bhkd->bhqk', q, k) * scale
            mask = jnp.tril(jnp.ones((s, s), dtype=bool))
            scores = jnp.where(mask, scores, jnp.finfo(scores.dtype).min)
            attn = jax.nn.softmax(scores, axis=-1)
            out = jnp.einsum('bhqk,bhkd->bhqd', attn, v)
            out = out.transpose(0, 2, 1, 3).reshape(b, s, d)
            return (out @ W_o.T, ckv)
        return _reference_tuple_inner(x, W_dq, W_uq, W_qr, W_dkv, W_ukv, W_kr, W_o, q_ln_g, q_ln_b, kv_ln_g, kv_ln_b)[0]

    def _L0_ffn_ref(x, gate_Wk, gate_bk, expert_queries, Wqkv, bqkv, Wo, bo, g1, be1, W1, bf1, W2, bf2, g2, be2):
        import jax, jax.numpy as jnp
        import numpy as np
        B, S, D, F, E, K, H = (4, 256, 128, 512, 8, 2, 8)
        HEAD_DIM = D // H

        def _layernorm(x, g, b):
            m = x.mean(-1, keepdims=True)
            v = ((x - m) ** 2).mean(-1, keepdims=True)
            return (x - m) * jax.lax.rsqrt(v + 1e-05) * g + b

        def _expert(x, Wqkv, bqkv, Wo, bo, g1, be1, W1, bf1, W2, bf2, g2, be2):
            b, s, d = x.shape
            qkv = x @ Wqkv.T + bqkv
            q, k, v = jnp.split(qkv, 3, axis=-1)
            to_heads = lambda t: t.reshape(b, s, H, HEAD_DIM).transpose(0, 2, 1, 3)
            q, k, v = (to_heads(q), to_heads(k), to_heads(v))
            scale = 1.0 / np.sqrt(HEAD_DIM).astype(np.float32)
            attn = jax.nn.softmax(jnp.einsum('bhqd,bhkd->bhqk', q * scale, k), axis=-1)
            ctx = jnp.einsum('bhqk,bhkd->bhqd', attn, v).transpose(0, 2, 1, 3).reshape(b, s, d)
            ctx = ctx @ Wo.T + bo
            x = _layernorm(x + ctx, g1, be1)
            h = jax.nn.gelu(x @ W1.T + bf1, approximate=False)
            h = jax.nn.gelu(h @ W2.T + bf2, approximate=False)
            return _layernorm(x + h, g2, be2)
        keys = x @ gate_Wk.T + gate_bk
        scores = jnp.einsum('bsd,ed->bse', keys, expert_queries) * D ** (-0.5)
        probs = jax.nn.softmax(scores, axis=-1)
        _, idx = jax.lax.top_k(probs, K)
        mask = jax.nn.one_hot(idx, E, dtype=probs.dtype).sum(-2)
        gated = probs * mask
        gated = gated / (gated.sum(-1, keepdims=True) + 1e-09)
        eo = jax.vmap(_expert, in_axes=(None,) + (0,) * 12)(x, Wqkv, bqkv, Wo, bo, g1, be1, W1, bf1, W2, bf2, g2, be2)
        return jnp.einsum('ebsd,bse->bsd', eo, gated)
    h = _L0_tok_ref(x, L0_tok_W, L0_tok_b, L0_tok_gamma, L0_tok_beta)
    h = h + _L0_attn_ref(_layernorm(h, axis=-1), L0_attn_W_dq, L0_attn_W_uq, L0_attn_W_qr, L0_attn_W_dkv, L0_attn_W_ukv, L0_attn_W_kr, L0_attn_W_o, L0_attn_q_ln_g, L0_attn_q_ln_b, L0_attn_kv_ln_g, L0_attn_kv_ln_b)
    h = h + _L0_ffn_ref(_layernorm(h, axis=-1), L0_ffn_gate_Wk, L0_ffn_gate_bk, L0_ffn_expert_queries, L0_ffn_Wqkv, L0_ffn_bqkv, L0_ffn_Wo, L0_ffn_bo, L0_ffn_g1, L0_ffn_be1, L0_ffn_W1, L0_ffn_bf1, L0_ffn_W2, L0_ffn_bf2, L0_ffn_g2, L0_ffn_be2)
    return h

_drawn_inputs = setup_inputs


def setup_inputs(seed=0):
    import zlib

    import numpy as np

    out = dict(_drawn_inputs(seed))
    spreads = {'L0_tok_gamma': (1.0, 0.2),
     'L0_tok_beta': (0.0, 0.1),
     'L0_attn_q_ln_g': (1.0, 0.6),
     'L0_attn_q_ln_b': (0.0, 0.8),
     'L0_attn_kv_ln_g': (1.0, 0.6),
     'L0_attn_kv_ln_b': (0.0, 0.8),
     'L0_ffn_gate_bk': (0.0, 0.1),
     'L0_ffn_bqkv': (0.0, 0.8),
     'L0_ffn_bo': (0.0, 0.486),
     'L0_ffn_g1': (1.0, 0.2),
     'L0_ffn_be1': (0.0, 0.1),
     'L0_ffn_bf1': (0.0, 0.8),
     'L0_ffn_bf2': (0.0, 0.444),
     'L0_ffn_g2': (1.0, 0.2),
     'L0_ffn_be2': (0.0, 0.1)}
    factors = {'L0_tok_b': 5.902,
     'L0_attn_W_dq': 8.0,
     'L0_attn_W_uq': 8.0,
     'L0_attn_W_qr': 8.0,
     'L0_attn_W_dkv': 8.0,
     'L0_attn_W_ukv': 8.0,
     'L0_attn_W_kr': 8.0,
     'L0_attn_W_o': 8.0,
     'L0_ffn_Wqkv': 8.0,
     'L0_ffn_Wo': 7.098,
     'L0_ffn_W1': 5.875,
     'L0_ffn_W2': 5.28}
    for name, (base, spread) in spreads.items():
        noise = np.random.default_rng([zlib.crc32(name.encode()), seed]).standard_normal(out[name].shape)
        drawn = base * np.exp(spread * noise) if base else spread * noise
        out[name] = jnp.asarray(drawn.astype(out[name].dtype))
    for name, factor in factors.items():
        out[name] = (out[name] * factor).astype(out[name].dtype)
    return out
```

```python
from contextlib import ExitStack

import concourse.bass as bass
import concourse.mybir as mybir
import numpy as np

ALU = mybir.AluOpType
ACT = mybir.ActivationFunctionType
AX = mybir.AxisListType
F32 = mybir.dt.float32
BF16 = mybir.dt.bfloat16

B, T_IN, D_IN, CTX = 128, 125, 40, 5
T = T_IN - CTX + 1
D = 128
H, DH = 8, 16
G = 4
NQ = B // G
C = G * T
E, F = 8, 512
FC = F // D
QP, KVP = D // 2, 2 * D // 3
CAT = QP + KVP
ROPE = D // 8
SHIFTS = (3, 2)
HP = 32
HG = 4
VW = H * D
UNITS = E + 1
STEPS = UNITS * G
EPS = 1e-5
MASKED = -1e30
MLA_SCALE = float((DH + ROPE // H) ** -0.5)
EXP_SCALE = float(DH ** -0.5)
GATE_SCALE = float(D ** -0.5)

COLS = ("conv_b", "gamma", "beta", "gate_b", "q_g", "q_b", "kv_g", "kv_b")
ECOLS = ("bq", "bk", "bf1_0", "bf1_1", "bf1_2", "bf1_3", "bf2", "g1", "be1", "bv_0", "bv_1")

CONSTS = (
    ("conv_w", 2 * D), ("wq", E * D), ("wk", E * D), ("wv", E * D), ("wo", E * 2 * D),
    ("w1", E * F), ("w2", E * F), ("mla_cat", CAT), ("mla_uq", D), ("mla_uk", D), ("mla_uv", D),
    ("mla_rope", 4 * ROPE), ("mla_wo", 2 * D), ("gate_w", D), ("gate_q", E), ("cols", len(COLS)),
    ("ecols", len(ECOLS) * E), ("bo_rows", E * D), ("g2_rows", E * D), ("be2", D), ("ident", D),
    ("causal", 2 * T), ("rope_tab", 2 * C), ("tri", E * E),
)


def build_program(nc, args, x_dram, out):
    with ExitStack() as ctx:
        def sb(name, cols, dt=F32):
            return ctx.enter_context(nc.sbuf_tensor(name, [128, cols], dt))

        class Signal:

            def __init__(self, name, per_group):
                self.sem = ctx.enter_context(nc.semaphore(name))
                self.n = per_group

            def at(self, q, k):
                return q * self.n + (max(k, 0) if isinstance(k, int) else k)

        const = {name: sb(name, n) for name, n in CONSTS}
        c_ = const
        ident, tri, rope_tab = const["ident"], const["tri"], const["rope_tab"]
        col = {n: const["cols"][:, i:i + 1] for i, n in enumerate(COLS)}
        ident_b = sb("ident_b", D, BF16)
        causal_b = sb("causal_b", 2 * T, BF16)
        minus_half = sb("minus_half", 2 * G)

        x1T = sb("x1T", E * C)
        qr_blk = x1T[0:ROPE, 0:H * C]
        x_win = [[sb("x_win0", C), sb("x_win1", C)], [x1T[:, 0:C], x1T[:, C:2 * C]]]
        relu_x = [sb("relu_x", C), x1T[:, 2 * C:3 * C]]
        conv_stats = sb("conv_stats", NQ * 6)
        bn = sb("bn", 8)
        h_tok, x_tok, z_tok = (sb(n, G * D) for n in ("h_tok", "x_tok", "z_tok"))
        s_tok = w_tok = h_tok
        acc = sb("acc", G * D)
        x0T, xT = sb("x0T", C), sb("xT", C)
        y2, yT = sb("y2", C), [sb("yT0", C), sb("yT1", C)]
        cqT, ckvT, h_bn = y2, yT[0], yT[1]
        keysT, gT = cqT, x0T
        qrT, krT = sb("qrT", C), sb("krT", C)
        q_sb, k_sb = [sb("q_sb0", C), sb("q_sb1", C)], [sb("k_sb0", C), sb("k_sb1", C)]
        q_blk = [sb("q_blk0", H * C), sb("q_blk1", H * C)]
        v_pad = [sb("v_pad0", G * VW), sb("v_pad1", G * VW)]
        probs = [sb("probs0", H * T), sb("probs1", H * T)]
        rope_a, rope_b = probs[0][:, 0:C], probs[0][:, C:2 * C]
        z_cat = probs[1]
        neg_max = [sb("neg_max0", H, BF16), sb("neg_max1", H, BF16)]
        recip, recip_sh = sb("recip", 2 * T), sb("recip_sh", 2 * T)
        h1T = sb("h1T", FC * C)
        ctx_pad = [h1T[:, 0:2 * C], h1T[:, 2 * C:4 * C]]
        st6, mv, veps, rstd = sb("st6", 2 * G * 6), sb("mv", 2 * G * 2), sb("veps", 2 * G), sb("rstd", 2 * G)
        g_max, g_sum, g_rec = sb("g_max", G), sb("g_sum", G), sb("g_rec", G)
        g_d, g_e, g_p, g_rank, g_mask = (sb(n, G * E) for n in ("g_d", "g_e", "g_p", "g_rank", "g_mask"))
        g_gt, g_ge = sb("g_gt", G * E * E), sb("g_ge", G * E * E)
        gated, rg = sb("gated", G * E), sb("rg", G)

        psum = ctx.enter_context(nc.psum_tensor("psum", [128, 8, 512], F32))

        def sig(name, per_group=1):
            return Signal(name, per_group)

        consts_in, zeroed, setup_dve, setup_pe, setup_rs = (sig(n) for n in (
            "consts_in", "zeroed", "setup_dve", "setup_pe", "setup_rs"))
        s_win = [sig("s_win0"), sig("s_win1")]
        s_conv = [sig("s_conv0"), sig("s_conv1")]
        s_relu = [sig("s_relu0"), sig("s_relu1")]
        s_bnst = [sig("s_bnst0"), sig("s_bnst1")]

        x_in, conv_done, relu_done, hbn_done = sig("x_in", 16 * CTX), sig("conv_done"), sig("relu_done"), sig("hbn_done")
        hbnT_done, z0_done, z0T_done, x0T_done = sig("hbnT_done"), sig("z0_done"), sig("z0T_done"), sig("x0T_done")
        cat_done, zcat_done, catT_done, catT_out = sig("cat_done"), sig("zcat_done"), sig("catT_done"), sig("catT_out", 2)
        mla_proj, rope_done = sig("mla_proj", 4), sig("rope_done", 2)
        qr_zero = sig("qr_zero")
        qr_blk_in = sig("qr_blk_in", 16 * H)
        z1_done, z1T_done, xT_done = sig("z1_done"), sig("z1T_done"), sig("xT_done")
        keys_done, keys_out, gscore_done, gd_done, ge_done, gated_done, gTT_done, gT_done, be2_done, acc_init = (sig(n) for n in (
            "keys_done", "keys_out", "gscore_done", "gd_done", "ge_done", "gated_done", "gTT_done", "gT_done",
            "be2_done", "acc_init"))
        q_proj, k_proj, v_proj = sig("q_proj", E), sig("k_proj", E), sig("v_proj", E)
        q_out, k_out, v_out = sig("q_out", UNITS), sig("k_out", UNITS), sig("v_out", UNITS)
        blk_in = [sig("blk_in0", 16 * H * 5), sig("blk_in1", 16 * H * 4)]
        a_done, max_done, b_done, exp_done, av_done, rec_done, shuf_done, norm_done = (sig(n, STEPS) for n in (
            "a_done", "max_done", "b_done", "exp_done", "av_done", "rec_done", "shuf_done", "norm_done"))
        wo_done, res_done = sig("wo_done", UNITS), sig("res_done", UNITS)
        NORMS = 3 + 2 * E
        stats_done, aggr_done, veps_done, rstd_done = (sig(n, NORMS) for n in (
            "stats_done", "aggr_done", "veps_done", "rstd_done"))
        sadd_done = sig("sadd_done", E)
        zs_done, zsT_done, x1T_done = sig("zs_done", E), sig("zsT_done", E), sig("x1T_done", E)
        up_done, gelu1_done = sig("up_done", E * FC), sig("gelu1_done", E * FC)
        down_done, gelu2_done, y_done, yT_done, rg_done, w_done, acc_done = (sig(n, E) for n in (
            "down_done", "gelu2_done", "y_done", "yT_done", "rg_done", "w_done", "acc_done"))
        gchain, out_sent = sig("gchain", 15), sig("out_sent", 16)

        def tok(tile, b, width=D):
            return tile[0:T, b * width:(b + 1) * width]

        def seq(tile, b, parts=128, base=0):
            return tile[0:parts, base + b * T:base + (b + 1) * T]

        def high(ap):
            return ap.bitcast(BF16).rearrange("p (n two) -> p n two", two=2)[:, :, 1]

        def heads(tile, half, b, parts=128):
            return tile[0:parts, half * HG * C:(half + 1) * HG * C].rearrange("p (h c) -> p h c", h=HG)[:, :, b * T:(b + 1) * T]

        def bank(i, parts=128, cols=C):
            return psum[0:parts, i, 0:cols]

        def ecol(name, e):
            i = ECOLS.index(name)
            return const["ecols"][:, i * E + e:i * E + e + 1]

        def wslice(name, e):
            return const[name][:, e * D:(e + 1) * D]

        def over_experts(body):
            for e in range(E):
                body(e, (e + 1) % 2, e == 0, e == E - 1)

        def blk_count(unit):
            return 16 * H * (unit // 2 + 1)

        def wait_apart(eng, sem, value):
            eng.wait_ge(sem, value)
            eng.nop(nofuse=True)

        block = ctx.enter_context(nc.Block())

        def load_windows(eng, q, tiles, sem):
            for i in range(CTX):
                j, r = (0, i) if i < SHIFTS[0] else (1, i - SHIFTS[0])
                dst = tiles[j][r * D_IN:(r + 1) * D_IN, :].rearrange("p (g t) -> p g t", g=G)
                eng.dma_start(dst, x_dram[:, bass.ds(q * G, G), i:i + T]).then_inc(sem, 16)

        @block.sync
        def _(sp):
            for name, n in CONSTS:
                sp.dma_start(const[name][:, :], args[name]).then_inc(consts_in.sem, 16)
            with sp.Fori(0, NQ // 2) as i:
                for p in range(2):
                    sp.wait_ge(s_conv[p].sem, i)
                    load_windows(sp, 2 * i + p, x_win[p], s_win[p].sem)

            def spread_q(q, unit):
                par = unit % 2
                wait_apart(sp, q_out.sem, q_out.at(q, unit + 1))
                wait_apart(sp, b_done.sem, b_done.at(q, (unit - 1) * G))
                for h in range(H):
                    sp.dma_start(q_blk[par][h * DH:(h + 1) * DH, h * C:(h + 1) * C],
                                 q_sb[par][h * DH:(h + 1) * DH, :]).then_inc(blk_in[par].sem, 16)

            sp.wait_ge(s_conv[0].sem, NQ // 2)
            with sp.Fori(0, NQ) as q:
                wait_apart(sp, conv_done.sem, conv_done.at(q, 0))
                load_windows(sp, q, x_win[0], x_in.sem)
                spread_q(q, 0)
                wait_apart(sp, rope_done.sem, rope_done.at(q, 1))
                wait_apart(sp, qr_zero.sem, qr_zero.at(q, 1))
                for h in range(H):
                    r = ROPE // H
                    sp.dma_start(qr_blk[h * r:(h + 1) * r, h * C:(h + 1) * C],
                                 qrT[h * r:(h + 1) * r, :]).then_inc(qr_blk_in.sem, 16)
                for unit in range(1, UNITS):
                    spread_q(q, unit)

        @block.tensor
        def _(pe):
            def conv(tiles, dst):
                for j, s in enumerate(SHIFTS):
                    m = pe.matmul(dst, c_["conv_w"][0:s * D_IN, j * D:(j + 1) * D], tiles[j][0:s * D_IN, :],
                                  start=j == 0, stop=j == 1)
                return m

            pe.wait_ge(consts_in.sem, 16 * len(CONSTS))
            for e in range(E):
                for g in range(2):
                    m = pe.matmul(psum[:, 2 + e // 4, (e % 4) * D:(e % 4 + 1) * D],
                                  const["ecols"][:, (9 + g) * E + e:(9 + g) * E + e + 1].to_broadcast([128, 128]),
                                  const["wo"][:, (2 * e + g) * D:(2 * e + g + 1) * D], start=g == 0, stop=g == 1)
            m.then_inc(setup_pe.sem, 1)
            with pe.Fori(0, NQ // 2) as i:
                for p in range(2):
                    pe.wait_ge(s_win[p].sem, 16 * CTX * i + 16 * CTX)
                    pe.wait_ge(s_relu[p].sem, i)
                    conv(x_win[p], bank(p)).then_inc(s_conv[p].sem, 1)

            def score_max(q, unit, b, par, step):
                pe.wait_ge(max_done.sem, max_done.at(q, step))
                mla = unit == 0
                for h in range(H):
                    dst = psum[0:T, h // HG, (h % HG) * T:(h % HG + 1) * T]
                    first = h % HG == 0
                    m = pe.matmul(dst, high(q_blk[par][:, h * C + b * T:h * C + (b + 1) * T]),
                                  high(seq(k_sb[par], b)), start=first or not mla, stop=True, skip_group_check=True)
                    if mla:
                        m = pe.matmul(dst, high(qr_blk[0:ROPE, h * C + b * T:h * C + (b + 1) * T]),
                                      high(seq(krT, b, ROPE)), start=False, stop=True, skip_group_check=True)
                if mla:
                    for half in range(2):
                        m = pe.matmul(psum[0:T, half, 0:C], ident_b[0:T, 0:T],
                                      causal_b[0:T, 0:T].rearrange("p (o k) -> p o k", o=1).to_broadcast([T, HG, T]),
                                      start=False, stop=True, skip_group_check=True)
                m.then_inc(a_done.sem, 1)

            def score_exp(q, unit, b, par, step):
                pe.wait_ge(exp_done.sem, exp_done.at(q, step))
                mla = unit == 0
                for half in range(2):
                    pe.matmul(psum[0:T, 2 + half, 0:C], seq(k_sb[par], b), heads(q_blk[par], half, b),
                              start=True, stop=True, skip_group_check=True)
                    if mla:
                        pe.matmul(psum[0:T, 2 + half, 0:C], seq(krT, b, ROPE), heads(qr_blk, half, b, ROPE),
                                  start=False, stop=True, skip_group_check=True)
                        pe.matmul(psum[0:T, 2 + half, 0:C], ident_b[0:T, 0:T],
                                  causal_b[0:T, T:2 * T].rearrange("p (o k) -> p o k", o=1).to_broadcast([T, HG, T]),
                                  start=False, stop=True, skip_group_check=True)
                pe.wait_ge(max_done.sem, max_done.at(q, step) + 1)
                for h in range(H):
                    m = pe.matmul(psum[0:T, 2 + h // HG, (h % HG) * T:(h % HG + 1) * T],
                                  neg_max[b % 2][0:T, h:h + 1].to_broadcast([T, T]), ident_b[0:T, 0:T],
                                  start=False, stop=True, skip_group_check=True)
                m.then_inc(b_done.sem, 1)

            def weigh(q, b, par, step):
                pe.wait_ge(exp_done.sem, exp_done.at(q, step) + 1)
                pe.wait_ge(norm_done.sem, norm_done.at(q, step))
                for h in range(H):
                    g, j = h // HG, h % HG
                    m = pe.matmul(psum[:, 7, g * T:(g + 1) * T],
                                  v_pad[par][0:T, b * VW + h * D:b * VW + (h + 1) * D],
                                  probs[b % 2][0:T, h * T:(h + 1) * T], start=j == 0, stop=j == HG - 1)
                m.then_inc(av_done.sem, 1)

            def out_proj(q, unit, par, w, e):
                pe.wait_ge(norm_done.sem, norm_done.at(q, (unit + 1) * G))
                for b in range(G):
                    for g in range(2):
                        m = pe.matmul(psum[0:T, 6, b * D:(b + 1) * D],
                                      ctx_pad[par][:, g * C + b * T:g * C + (b + 1) * T],
                                      const[w][:, (2 * e + g) * D:(2 * e + g + 1) * D], start=g == 0, stop=g == 1)
                m.then_inc(wo_done.sem, 1)

            def to_feature(src, i, sem, parts=D, base=0, width=D):
                for b in range(G):
                    m = pe.transpose(psum[0:parts, i, b * T:(b + 1) * T],
                                     src[0:T, b * width + base:b * width + base + parts], ident[0:T, 0:T])
                if sem is not None:
                    m.then_inc(sem, 1)
                return m

            def to_token(src, i, sem):
                for b in range(G):
                    m = pe.transpose(psum[0:T, i, b * D:(b + 1) * D], seq(src, b), ident[:, :])
                m.then_inc(sem, 1)

            def qk_proj(q, e):
                pe.wait_ge(v_out.sem, v_out.at(q, 1) + e)
                pe.matmul(bank(4), wslice("wq", e), xT[:, :], start=True, stop=True).then_inc(q_proj.sem, 1)
                pe.matmul(bank(5), wslice("wk", e), xT[:, :], start=True, stop=True).then_inc(k_proj.sem, 1)

            def v_proj_(q, e):
                pe.wait_ge(q_out.sem, q_out.at(q, 2) + e)
                for b in range(G):
                    m = pe.matmul(psum[0:T, 4, b * D:(b + 1) * D], seq(xT, b), wslice("wv", e), start=True, stop=True)
                m.then_inc(v_proj.sem, 1)

            with pe.Fori(0, NQ) as q:
                pe.wait_ge(x_in.sem, x_in.at(q, 16 * CTX))
                pe.wait_ge(gelu2_done.sem, gelu2_done.at(q, 0))
                conv(x_win[0], bank(4)).then_inc(conv_done.sem, 1)
                pe.wait_ge(hbn_done.sem, hbn_done.at(q, 1))
                pe.wait_ge(w_done.sem, w_done.at(q, 0))
                to_token(h_bn, 6, hbnT_done.sem)
                pe.wait_ge(z0_done.sem, z0_done.at(q, 1))
                to_feature(z_tok, 5, z0T_done.sem)
                pe.wait_ge(x0T_done.sem, x0T_done.at(q, 1))
                for b in range(G):
                    m = pe.matmul(psum[0:T, b // 2, (b % 2) * CAT:(b % 2 + 1) * CAT], seq(x0T, b), c_["mla_cat"][:, :],
                                  start=True, stop=True)
                m.then_inc(cat_done.sem, 1)
                wait_apart(pe, zcat_done.sem, zcat_done.at(q, 1))
                to_feature(z_cat, 4, None, QP, 0, CAT)
                to_feature(z_cat, 5, catT_done.sem, KVP, QP, CAT)
                pe.wait_ge(catT_out.sem, catT_out.at(q, 2))
                pe.matmul(bank(2), c_["mla_uq"][0:QP, :], cqT[0:QP, :], start=True, stop=True)
                pe.matmul(bank(3), c_["mla_uk"][0:KVP, :], ckvT[0:KVP, :], start=True, stop=True).then_inc(mla_proj.sem, 1)
                for j in range(2):
                    m = pe.matmul(bank(6 + j, ROPE), c_["mla_rope"][0:QP, j * ROPE:(j + 1) * ROPE], cqT[0:QP, :],
                                  start=True, stop=True)
                m.then_inc(mla_proj.sem, 1)
                for j in range(2):
                    m = pe.matmul(bank(j, ROPE), c_["mla_rope"][:, (2 + j) * ROPE:(3 + j) * ROPE], x0T[:, :],
                                  start=True, stop=True)
                m.then_inc(mla_proj.sem, 1)
                for b in range(G):
                    m = pe.matmul(psum[0:T, 4, b * D:(b + 1) * D], seq(ckvT, b, KVP), c_["mla_uv"][0:KVP, :],
                                  start=True, stop=True)
                m.then_inc(mla_proj.sem, 1)
                pe.wait_ge(blk_in[0].sem, blk_in[0].at(q, 16 * H))
                pe.wait_ge(qr_blk_in.sem, qr_blk_in.at(q, 16 * H))
                pe.wait_ge(k_out.sem, k_out.at(q, 1))
                pe.wait_ge(rope_done.sem, rope_done.at(q, 2))
                pe.wait_ge(v_out.sem, v_out.at(q, 1))
                score_max(q, 0, 0, 0, 0)
                for b in range(G):
                    if b + 1 < G:
                        score_max(q, 0, b + 1, 0, b + 1)
                    score_exp(q, 0, b, 0, b)
                    if b:
                        weigh(q, b - 1, 0, b - 1)
                weigh(q, G - 1, 0, G - 1)
                out_proj(q, 0, 0, "mla_wo", 0)
                pe.wait_ge(z1_done.sem, z1_done.at(q, 1))
                to_feature(x_tok, 5, z1T_done.sem)
                pe.wait_ge(xT_done.sem, xT_done.at(q, 1))
                pe.matmul(bank(2), c_["gate_w"][:, :], xT[:, :], start=True, stop=True).then_inc(keys_done.sem, 1)
                qk_proj(q, 0)
                v_proj_(q, 0)
                pe.wait_ge(keys_out.sem, keys_out.at(q, 1))
                for b in range(G):
                    m = pe.matmul(psum[0:T, 6, b * E:(b + 1) * E], seq(keysT, b), c_["gate_q"][:, :], start=True, stop=True)
                m.then_inc(gscore_done.sem, 1)
                pe.wait_ge(blk_in[1].sem, blk_in[1].at(q, 16 * H))
                pe.wait_ge(k_out.sem, k_out.at(q, 2))
                score_max(q, 1, 0, 1, G)

                def attend(e, par, first, last):
                    unit, s0 = e + 1, (e + 1) * G
                    pe.wait_ge(v_out.sem, v_out.at(q, unit + 1))
                    for b in range(G):
                        if b + 1 < G:
                            score_max(q, unit, b + 1, par, s0 + b + 1)
                        elif not last:
                            nxt = unit + 1
                            pe.wait_ge(blk_in[1 - par].sem, blk_in[1 - par].at(q, blk_count(nxt)))
                            pe.wait_ge(k_out.sem, k_out.at(q, nxt + 1))
                            score_max(q, nxt, 0, 1 - par, s0 + G)
                        score_exp(q, unit, b, par, s0 + b)
                        if b:
                            weigh(q, b - 1, par, s0 + b - 1)
                        elif not first:
                            weigh(q, G - 1, 1 - par, s0 - 1)
                        if b == 0 and not last:
                            if not first:
                                pe.wait_ge(x1T_done.sem, x1T_done.at(q, e - 1))
                            qk_proj(q, e + 1)
                        if b == 1:
                            if not last:
                                v_proj_(q, e + 1)
                            if not first:
                                out_proj(q, e, 1 - par, "wo", e - 1)
                            else:
                                gate_out()
                        if b == 3 and not first:
                            z_out(e - 1)

                def gate_out():
                    pe.wait_ge(gated_done.sem, gated_done.at(q, 1))
                    for b in range(G):
                        m = pe.transpose(psum[0:E, 6, b * T:(b + 1) * T], gated[0:T, b * E:(b + 1) * E], ident[0:T, 0:T])
                    m.then_inc(gTT_done.sem, 1)
                    pe.wait_ge(gT_done.sem, gT_done.at(q, 1))
                    for b in range(G):
                        m = pe.matmul(psum[0:T, 6, b * D:(b + 1) * D], seq(gT, b, E), c_["be2"][0:E, :], start=True, stop=True)
                    m.then_inc(be2_done.sem, 1)
                    pe.wait_ge(acc_init.sem, acc_init.at(q, 1))

                def z_out(e):
                    pe.wait_ge(zs_done.sem, zs_done.at(q, e + 1))
                    pe.wait_ge(k_out.sem, k_out.at(q, min(e + 4, UNITS)))
                    pe.wait_ge(x1T_done.sem, x1T_done.at(q, e))
                    to_feature(z_tok, 5, zsT_done.sem)

                over_experts(attend)
                weigh(q, G - 1, 0, STEPS - 1)
                out_proj(q, E, 0, "wo", E - 1)
                z_out(E - 1)

                def up(e, c):
                    pe.matmul(bank(c), const["w1"][:, e * F + c * D:e * F + (c + 1) * D], x1T[:, e * C:(e + 1) * C],
                              start=True, stop=True).then_inc(up_done.sem, 1)

                def tail(e, par):
                    pe.wait_ge(y_done.sem, y_done.at(q, e + 1))
                    to_token(yT[par], 6 + par, yT_done.sem)

                def hidden(e, par, first, last):
                    for c in range(FC):
                        pe.wait_ge(gelu1_done.sem, gelu1_done.at(q, e * FC + c + 1))
                        m = pe.matmul(bank(4 + par), const["w2"][:, e * F + c * D:e * F + (c + 1) * D],
                                      h1T[:, c * C:(c + 1) * C], start=c == 0, stop=c == FC - 1)
                        if c == FC - 1:
                            m.then_inc(down_done.sem, 1)
                        if not last:
                            up(e + 1, c)
                        if c == 1 and not first:
                            tail(e - 1, 1 - par)

                pe.wait_ge(x1T_done.sem, x1T_done.at(q, E))
                for c in range(FC):
                    up(0, c)
                over_experts(hidden)
                tail(E - 1, 0)

        @block.scalar
        def _(act):
            act.wait_ge(consts_in.sem, 16 * len(CONSTS))
            with act.Fori(0, NQ // 2) as i:
                for p in range(2):
                    act.wait_ge(s_conv[p].sem, i + 1)
                    act.wait_ge(s_bnst[p].sem, i)
                    act.activation(relu_x[p][:, :], bank(p), ACT.Relu, bias=col["conv_b"]).then_inc(s_relu[p].sem, 1)

            def exps(q, b, step, scale):
                act.wait_ge(b_done.sem, b_done.at(q, step) + 1)
                act.wait_ge(av_done.sem, av_done.at(q, step - 1))
                act.activation(probs[b % 2][0:T, :].rearrange("p (a c) -> p a c", a=2), psum[0:T, 2:4, 0:C], ACT.Exp,
                               scale=scale).then_inc(exp_done.sem, 1)

            def v_evac(q, par, unit):
                for b in range(G):
                    dst = v_pad[par][0:T, b * VW:(b + 1) * VW].rearrange("p (g x) -> p g x", g=2)
                    for g in range(2):
                        d = dst[:, g, :].rearrange("p (j y) -> p j y", j=HG)
                        m = act.activation(
                            bass.AP(tensor=d.tensor, offset=d.offset, ap=[list(d.ap[0]), [D + HP, HG], [1, DH]]),
                            psum[0:T, 4, b * D + g * HG * DH:b * D + (g + 1) * HG * DH].rearrange("p (j d) -> p j d", j=HG),
                            ACT.Copy)
                m.then_inc(v_out.sem, 1)

            for p in range(2):
                act.wait_ge(s_bnst[p].sem, NQ // 2)
            with act.Fori(0, NQ) as q:
                act.wait_ge(conv_done.sem, conv_done.at(q, 1))
                act.activation(relu_x[0][:, :], bank(4), ACT.Relu, bias=col["conv_b"]).then_inc(relu_done.sem, 1)
                act.wait_ge(z0T_done.sem, z0T_done.at(q, 1))
                act.activation(x0T[:, :], bank(5), ACT.Copy).then_inc(x0T_done.sem, 1)
                act.wait_ge(catT_done.sem, catT_done.at(q, 1))
                for i, (dst, n, k) in enumerate(((cqT, "q", QP), (ckvT, "kv", KVP))):
                    act.activation(dst[0:k, :], bank(4 + i, k), ACT.Identity, bias=col[n + "_b"][0:k],
                                   scale=col[n + "_g"][0:k]).then_inc(catT_out.sem, 1)
                act.wait_ge(mla_proj.sem, mla_proj.at(q, 1))
                act.activation(q_sb[0][:, :], bank(2), ACT.Copy).then_inc(q_out.sem, 1)
                act.wait_ge(mla_proj.sem, mla_proj.at(q, 4))
                v_evac(q, 0, 0)
                for b in range(G):
                    exps(q, b, b, MLA_SCALE)
                act.wait_ge(z1T_done.sem, z1T_done.at(q, 1))
                act.activation(xT[:, :], bank(5), ACT.Copy).then_inc(xT_done.sem, 1)
                act.wait_ge(keys_done.sem, keys_done.at(q, 1))
                act.activation(keysT[:, :], bank(2), ACT.Identity, bias=col["gate_b"]).then_inc(keys_out.sem, 1)

                def q_evac(e, par):
                    act.wait_ge(q_proj.sem, q_proj.at(q, e + 1))
                    act.wait_ge(blk_in[par].sem, blk_in[par].at(q, blk_count(e + 1 - 2)))
                    act.activation(q_sb[par][:, :], bank(4), ACT.Identity, bias=ecol("bq", e)).then_inc(q_out.sem, 1)

                def v_out_(e, par):
                    act.wait_ge(v_proj.sem, v_proj.at(q, e + 1))
                    act.wait_ge(av_done.sem, av_done.at(q, e * G))
                    v_evac(q, par, e + 1)

                q_evac(0, 1)
                v_out_(0, 1)

                act.wait_ge(gd_done.sem, gd_done.at(q, 1))
                act.activation(g_e[0:T, :], g_d[0:T, :], ACT.Exp, scale=GATE_SCALE).then_inc(ge_done.sem, 1)

                def attend(e, par, first, last):
                    s0 = (e + 1) * G
                    for b in range(G):
                        exps(q, b, s0 + b, EXP_SCALE)
                        if b == 0 and not last:
                            q_evac(e + 1, 1 - par)
                        if b == 1 and not last:
                            v_out_(e + 1, 1 - par)
                        if b == 1 and first:
                            act.wait_ge(gTT_done.sem, gTT_done.at(q, 1))
                            act.activation(gT[0:E, :], bank(6, E), ACT.Copy).then_inc(gT_done.sem, 1)
                        if b == 3 and not first:
                            x1_out(e - 1)

                def x1_out(e):
                    act.wait_ge(zsT_done.sem, zsT_done.at(q, e + 1))
                    act.activation(x1T[:, e * C:(e + 1) * C], bank(5), ACT.Identity, bias=ecol("be1", e),
                                   scale=ecol("g1", e)).then_inc(x1T_done.sem, 1)

                over_experts(attend)
                x1_out(E - 1)

                def gelu1(e, c):
                    act.wait_ge(up_done.sem, up_done.at(q, e * FC + c + 1))
                    act.activation(h1T[:, c * C:(c + 1) * C], bank(c), ACT.Gelu,
                                   bias=ecol(f"bf1_{c}", e)).then_inc(gelu1_done.sem, 1)

                def hidden(e, par, first, last):
                    for c in range(FC):
                        if c == FC - 1:
                            act.wait_ge(down_done.sem, down_done.at(q, e + 1))
                            act.wait_ge(y_done.sem, y_done.at(q, e))
                            act.activation(y2[:, :], bank(4 + par), ACT.Gelu, bias=ecol("bf2", e)).then_inc(gelu2_done.sem, 1)
                        if not last:
                            gelu1(e + 1, c)

                for c in range(FC):
                    gelu1(0, c)
                over_experts(hidden)

        @block.vector
        def _(dve):
            for t_ in q_blk + v_pad:
                dve.memset(t_[:, :], 0.0)
            dve.memset(minus_half[:, :], -0.5).then_inc(setup_dve.sem, 1)
            dve.wait_ge(setup_dve.sem, 1)
            for t_ in v_pad:
                for b in range(G):
                    for h in range(H):
                        c0 = b * VW + h * D + (h % HG) * HP + DH
                        m = dve.memset(t_[:, c0:c0 + DH], 1.0)
            m.then_inc(zeroed.sem, 1)
            dve.wait_ge(consts_in.sem, 16 * len(CONSTS))
            dve.tensor_copy(ident_b[:, :], ident[:, :])
            dve.tensor_copy(causal_b[:, :], const["causal"][:, :])
            dve.wait_ge(setup_pe.sem, 1)
            dve.tensor_tensor(const["bo_rows"][:, 0:4 * D], psum[:, 2, :], const["bo_rows"][:, 0:4 * D], ALU.add)
            dve.tensor_tensor(const["bo_rows"][:, 4 * D:], psum[:, 3, :], const["bo_rows"][:, 4 * D:],
                              ALU.add).then_inc(setup_dve.sem, 1)
            with dve.Fori(0, NQ // 2) as i:
                for p in range(2):
                    dve.wait_ge(s_relu[p].sem, i + 1)
                    dve.bn_stats(conv_stats[:, bass.ds((2 * i + p) * 6, 6)], relu_x[p][:, :]).then_inc(s_bnst[p].sem, 1)
            for p in range(2):
                dve.wait_ge(s_bnst[p].sem, NQ // 2)
            dve.bn_aggr(bn[:, 0:2], conv_stats[:, :]).then_inc(setup_dve.sem, 1)
            dve.wait_ge(setup_dve.sem, 3)
            dve.tensor_scalar(bn[:, 2:3], bn[:, 1:2], EPS, None, ALU.add).then_inc(setup_dve.sem, 1)
            dve.wait_ge(setup_rs.sem, 1)
            dve.tensor_scalar(bn[:, 4:5], bn[:, 3:4], col["gamma"], None, ALU.mult).then_inc(setup_dve.sem, 1)
            dve.wait_ge(setup_dve.sem, 5)
            dve.tensor_scalar(bn[:, 5:6], bn[:, 0:1], bn[:, 4:5], None, ALU.mult).then_inc(setup_dve.sem, 1)
            dve.wait_ge(setup_dve.sem, 6)
            dve.tensor_tensor(bn[:, 6:7], col["beta"], bn[:, 5:6], ALU.subtract).then_inc(setup_dve.sem, 1)
            dve.wait_ge(setup_dve.sem, 7)

            def norm_stats(q, n, sources, plus=None):
                m = len(sources)
                for i, src in enumerate(sources):
                    ins = dve.bn_stats(st6[0:T, 6 * i:6 * i + 6], src)
                ins.then_inc(stats_done.sem, 1)
                wait_apart(dve, stats_done.sem, stats_done.at(q, n) + 1)
                for i in range(m):
                    ins = dve.bn_aggr(mv[0:T, 2 * i:2 * i + 2], st6[0:T, 6 * i:6 * i + 6])
                ins.then_inc(aggr_done.sem, 1)
                dve.wait_ge(aggr_done.sem, aggr_done.at(q, n) + 1)
                dve.wait_ge(rstd_done.sem, rstd_done.at(q, n))
                dve.tensor_scalar(veps[0:T, 0:m], mv[0:T, 1:2 * m:2], EPS, None, ALU.add).then_inc(veps_done.sem, 1)

            def standardize(q, n, pairs):
                dve.wait_ge(rstd_done.sem, rstd_done.at(q, n) + 1)
                for i, (dst, src) in enumerate(pairs):
                    ins = dve.tensor_scalar(dst, src, mv[0:T, 2 * i:2 * i + 1], rstd[0:T, i:i + 1],
                                            ALU.subtract, ALU.mult)
                return ins

            def bank_tok(i, b):
                return psum[0:T, i, b * D:(b + 1) * D]

            def row_max(q, b, step):
                dve.wait_ge(a_done.sem, a_done.at(q, step) + 1)
                dve.wait_ge(b_done.sem, b_done.at(q, step - 1))
                dve.tensor_reduce(neg_max[b % 2][0:T, :].rearrange("p (a h) -> p a h", a=2),
                                  psum[0:T, 0:2, 0:C].rearrange("p a (h k) -> p a h k", h=HG),
                                  AX.X, ALU.max, negate=True).then_inc(max_done.sem, 1)

            def norm_ctx(q, b, par, step):
                dve.wait_ge(av_done.sem, av_done.at(q, step) + 1)
                dve.reciprocal(recip[:, :], psum[:, 7, 0:2 * T]).then_inc(rec_done.sem, 1)
                wait_apart(dve, rec_done.sem, rec_done.at(q, step) + 1)
                dve.stream_shuffle(recip_sh[:, :], recip[:, :],
                                   [DH + i % DH for i in range(HP)]).then_inc(shuf_done.sem, 1)
                dve.wait_ge(shuf_done.sem, shuf_done.at(q, step) + 1)
                dve.tensor_tensor(ctx_pad[par][:, :].rearrange("p (g c) -> p g c", g=2)[:, :, b * T:(b + 1) * T],
                                  psum[:, 7, 0:2 * T].rearrange("p (g t) -> p g t", g=2),
                                  recip_sh[:, :].rearrange("p (g t) -> p g t", g=2), ALU.mult).then_inc(norm_done.sem, 1)

            with dve.Fori(0, NQ) as q:
                dve.wait_ge(relu_done.sem, relu_done.at(q, 1))
                dve.tensor_scalar(h_bn[:, :], relu_x[0][:, :], bn[:, 4:5], bn[:, 6:7], ALU.mult,
                                  ALU.add).then_inc(hbn_done.sem, 1)
                dve.wait_ge(hbnT_done.sem, hbnT_done.at(q, 1))
                norm_stats(q, 0, [bank_tok(6, b) for b in range(G)])
                dve.tensor_copy(h_tok[0:T, :], psum[0:T, 6, :])
                standardize(q, 0, [(tok(z_tok, b), bank_tok(6, b)) for b in range(G)]).then_inc(z0_done.sem, 1)
                dve.wait_ge(cat_done.sem, cat_done.at(q, 1))
                pairs = []
                for b in range(G):
                    for o, w in ((0, QP), (QP, KVP)):
                        pairs.append((z_cat[0:T, b * CAT + o:b * CAT + o + w],
                                      psum[0:T, b // 2, (b % 2) * CAT + o:(b % 2) * CAT + o + w]))
                norm_stats(q, 1, [p[1] for p in pairs])
                standardize(q, 1, pairs).then_inc(zcat_done.sem, 1)
                dve.wait_ge(mla_proj.sem, mla_proj.at(q, 1))
                dve.tensor_copy(k_sb[0][:, :], bank(3)).then_inc(k_out.sem, 1)
                for j, (dst, bk) in enumerate(((qrT, 6), (krT, 0))):
                    dve.wait_ge(mla_proj.sem, mla_proj.at(q, 2 + j))
                    dve.tensor_tensor(rope_a[0:ROPE, :], bank(bk, ROPE), rope_tab[0:ROPE, 0:C], ALU.mult)
                    dve.tensor_tensor(rope_b[0:ROPE, :], bank(bk + 1, ROPE), rope_tab[0:ROPE, C:2 * C],
                                      ALU.mult).then_inc(gchain.sem, 1)
                    dve.wait_ge(gchain.sem, gchain.at(q, j + 1))
                    dve.tensor_tensor(dst[0:ROPE, :], rope_a[0:ROPE, :], rope_b[0:ROPE, :], ALU.add).then_inc(rope_done.sem, 1)
                    dve.wait_ge(rope_done.sem, rope_done.at(q, j + 1))
                row_max(q, 0, 0)
                for b in range(G):
                    if b + 1 < G:
                        row_max(q, b + 1, b + 1)
                    if b:
                        norm_ctx(q, b - 1, 0, b - 1)
                norm_ctx(q, G - 1, 0, G - 1)
                dve.wait_ge(wo_done.sem, wo_done.at(q, 1))
                dve.wait_ge(out_sent.sem, out_sent.at(q, 0))
                dve.tensor_tensor(acc[0:T, :], psum[0:T, 6, :], h_tok[0:T, :], ALU.add).then_inc(res_done.sem, 1)
                dve.wait_ge(res_done.sem, res_done.at(q, 1))
                norm_stats(q, 2, [tok(acc, b) for b in range(G)])
                standardize(q, 2, [(tok(x_tok, b), tok(acc, b)) for b in range(G)]).then_inc(z1_done.sem, 1)

                def k_evac(e, par):
                    dve.wait_ge(k_proj.sem, k_proj.at(q, e + 1))
                    dve.wait_ge(b_done.sem, b_done.at(q, e * G))
                    dve.tensor_scalar(k_sb[par][:, :], bank(5), ecol("bk", e), None, ALU.add).then_inc(k_out.sem, 1)

                k_evac(0, 1)

                step_no = [2]

                def link(ins):
                    step_no[0] += 1
                    ins.then_inc(gchain.sem, 1)
                    dve.wait_ge(gchain.sem, gchain.at(q, step_no[0]))

                def gate():
                    v3 = lambda t_: t_[0:T, :].rearrange("p (b e) -> p b e", b=G)
                    v4 = lambda t_: t_[0:T, :].rearrange("p (b e j) -> p b e j", b=G, e=E)
                    per_tok = lambda t_: t_[0:T, :].rearrange("p (b o) -> p b o", o=1).to_broadcast([T, G, E])
                    dve.wait_ge(gscore_done.sem, gscore_done.at(q, 1))
                    sc = psum[0:T, 6, 0:G * E].rearrange("p (b e) -> p b e", b=G)
                    link(dve.tensor_reduce(g_max[0:T, :], sc, AX.X, ALU.max))
                    dve.tensor_tensor(v3(g_d), sc, per_tok(g_max), ALU.subtract).then_inc(gd_done.sem, 1)
                    dve.wait_ge(ge_done.sem, ge_done.at(q, 1))
                    link(dve.tensor_reduce(g_sum[0:T, :], v3(g_e), AX.X, ALU.add))
                    link(dve.reciprocal(g_rec[0:T, :], g_sum[0:T, :]))
                    link(dve.tensor_tensor(v3(g_p), v3(g_e), per_tok(g_rec), ALU.mult))
                    p_j = g_p[0:T, :].rearrange("p (b o j) -> p b o j", b=G, o=1).to_broadcast([T, G, E, E])
                    p_e = g_p[0:T, :].rearrange("p (b e o) -> p b e o", b=G, o=1).to_broadcast([T, G, E, E])
                    lower = tri[0:T, :].rearrange("p (o e j) -> p o e j", o=1, e=E).to_broadcast([T, G, E, E])
                    dve.tensor_tensor(v4(g_gt), p_j, p_e, ALU.is_gt)
                    link(dve.tensor_tensor(v4(g_ge), p_j, p_e, ALU.is_equal))
                    link(dve.tensor_tensor(v4(g_ge), v4(g_ge), lower, ALU.mult))
                    link(dve.tensor_tensor(v4(g_gt), v4(g_gt), v4(g_ge), ALU.add))
                    link(dve.tensor_reduce(v3(g_rank), v4(g_gt), AX.X, ALU.add))
                    link(dve.tensor_scalar(g_mask[0:T, :], g_rank[0:T, :], 1.5, None, ALU.is_lt))
                    link(dve.tensor_tensor(g_mask[0:T, :], g_mask[0:T, :], g_p[0:T, :], ALU.mult))
                    link(dve.tensor_reduce(g_sum[0:T, :], v3(g_mask), AX.X, ALU.add))
                    link(dve.tensor_scalar(g_sum[0:T, :], g_sum[0:T, :], 1e-9, None, ALU.add))
                    link(dve.reciprocal(g_rec[0:T, :], g_sum[0:T, :]))
                    dve.tensor_tensor(v3(gated), v3(g_mask), per_tok(g_rec), ALU.mult).then_inc(gated_done.sem, 1)
                    assert step_no[0] == gchain.n

                def attend(e, par, first, last):
                    s0 = (e + 1) * G
                    for b in range(G):
                        if b + 1 < G or not last:
                            row_max(q, (b + 1) % G, s0 + b + 1)
                        if b:
                            norm_ctx(q, b - 1, par, s0 + b - 1)
                        elif not first:
                            norm_ctx(q, G - 1, 1 - par, s0 - 1)
                        if b == 0 and not last:
                            k_evac(e + 1, 1 - par)
                        if b == 0 and first:
                            gate()
                        if b == 1 and first:
                            dve.wait_ge(be2_done.sem, be2_done.at(q, 1))
                            dve.tensor_tensor(acc[0:T, :], psum[0:T, 6, :], acc[0:T, :], ALU.add).then_inc(acc_init.sem, 1)
                        if b == 1 and not first:
                            first_norm(e - 1)
                        if b == 2 and not first:
                            first_norm_out(e - 1)

                def first_norm(e):
                    bo = const["bo_rows"][0:T, e * D:(e + 1) * D].rearrange("p (o d) -> p o d", o=1).to_broadcast([T, G, D])
                    dve.wait_ge(wo_done.sem, wo_done.at(q, e + 2))
                    dve.tensor_tensor(s_tok[0:T, :].rearrange("p (b d) -> p b d", b=G),
                                      psum[0:T, 6, :].rearrange("p (b d) -> p b d", b=G), bo, ALU.add).then_inc(sadd_done.sem, 1)
                    dve.wait_ge(sadd_done.sem, sadd_done.at(q, e + 1))
                    dve.tensor_tensor(s_tok[0:T, :], s_tok[0:T, :], x_tok[0:T, :], ALU.add).then_inc(res_done.sem, 1)
                    dve.wait_ge(res_done.sem, res_done.at(q, e + 2))
                    norm_stats(q, 3 + e, [tok(s_tok, b) for b in range(G)])

                def first_norm_out(e):
                    dve.wait_ge(zsT_done.sem, zsT_done.at(q, e))
                    standardize(q, 3 + e, [(tok(z_tok, b), tok(s_tok, b)) for b in range(G)]).then_inc(zs_done.sem, 1)

                row_max(q, 0, G)
                over_experts(attend)
                norm_ctx(q, G - 1, 0, STEPS - 1)
                first_norm(E - 1)
                first_norm_out(E - 1)

                def hidden(e, par, first, last):
                    dve.wait_ge(gelu2_done.sem, gelu2_done.at(q, e + 1))
                    dve.wait_ge(yT_done.sem, yT_done.at(q, e - 1))
                    dve.tensor_tensor(yT[par][:, :], y2[:, :], x1T[:, e * C:(e + 1) * C], ALU.add).then_inc(y_done.sem, 1)
                    if not first:
                        second_norm(e - 1, 1 - par)

                def second_norm(e, par):
                    dve.wait_ge(yT_done.sem, yT_done.at(q, e + 1))
                    norm_stats(q, 3 + E + e, [bank_tok(6 + par, b) for b in range(G)])
                    g2 = const["g2_rows"][0:T, e * D:(e + 1) * D]
                    dve.wait_ge(acc_done.sem, acc_done.at(q, e))
                    for b in range(G):
                        ins = dve.scalar_tensor_tensor(tok(w_tok, b), bank_tok(6 + par, b), mv[0:T, 2 * b:2 * b + 1], g2,
                                                       ALU.subtract, ALU.mult)
                    ins.then_inc(w_done.sem, 1)
                    dve.wait_ge(rstd_done.sem, rstd_done.at(q, 3 + E + e) + 1)
                    dve.tensor_tensor(rg[0:T, :], rstd[0:T, 0:G],
                                      gated[0:T, :].rearrange("p (b e) -> p b e", b=G)[:, :, e],
                                      ALU.mult).then_inc(rg_done.sem, 1)
                    dve.wait_ge(rg_done.sem, rg_done.at(q, e + 1))
                    for b in range(G):
                        ins = dve.scalar_tensor_tensor(tok(acc, b), tok(w_tok, b), rg[0:T, b:b + 1], tok(acc, b),
                                                       ALU.mult, ALU.add)
                    ins.then_inc(acc_done.sem, 1)

                over_experts(hidden)
                second_norm(E - 1, 0)

        @block.gpsimd
        def _(pool):
            pool.wait_ge(zeroed.sem, 1)
            for p in range(2):
                pool.wait_ge(s_bnst[p].sem, NQ // 2)
            pool.wait_ge(setup_dve.sem, 4)
            pool.tensor_tensor(bn[:, 3:4], bn[:, 2:3], minus_half[:, 0:1], ALU.pow).then_inc(setup_rs.sem, 1)

            def power(q, n, m):
                pool.wait_ge(veps_done.sem, veps_done.at(q, n) + 1)
                pool.tensor_tensor(rstd[0:T, 0:m], veps[0:T, 0:m], minus_half[0:T, 0:m], ALU.pow).then_inc(rstd_done.sem, 1)

            with pool.Fori(0, NQ) as q:
                wait_apart(pool, y_done.sem, y_done.at(q, 0))
                pool.memset(qr_blk, 0.0).then_inc(qr_zero.sem, 1)
                power(q, 0, G)
                power(q, 1, 2 * G)
                power(q, 2, G)
                with pool.Fori(0, E) as e:
                    power(q, 3 + e, G)
                with pool.Fori(0, E) as e:
                    power(q, 3 + E + e, G)
                pool.wait_ge(acc_done.sem, acc_done.at(q, E))
                pool.dma_start(out[bass.ds(q * G, G), :, :].rearrange("g t d -> t g d"),
                               acc[0:T, :].rearrange("p (g d) -> p g d", g=G)).then_inc(out_sent.sem, 16)
            pool.wait_ge(out_sent.sem, 16 * NQ)


def layouts(x, n):
    f = np.float32

    def rows(*parts, cols):
        out = np.zeros((128, cols), f)
        at = 0
        for p in parts:
            out[:p.shape[0], at:at + p.shape[1]] = p
            at += p.shape[1]
        return out

    def pad_heads(w):
        w = w.reshape(2, HG, DH, -1)
        out = np.zeros((2, HG, HP, w.shape[-1]), f)
        out[:, :, :DH] = w
        return out.reshape(2, HG * HP, -1).transpose(1, 0, 2).reshape(HG * HP, -1)

    swap = np.arange(ROPE) ^ 1
    cut = SHIFTS[0] * D_IN
    wt = n["L0_tok_W"].T
    qkv = n["L0_ffn_Wqkv"].transpose(2, 0, 1).reshape(D, E, 3, D)
    bqkv = n["L0_ffn_bqkv"].reshape(E, 3, D)
    ukv = n["L0_attn_W_ukv"]
    bv = np.stack([pad_heads(bqkv[e, 2][:, None]) for e in range(E)])
    bf1 = n["L0_ffn_bf1"].reshape(E, FC, D)
    t = np.arange(T, dtype=f)
    sign = np.where(np.arange(ROPE) % 2 == 0, -1, 1).astype(f)[:, None]
    cos, sin = np.tile(np.cos(t), G)[None], np.tile(np.sin(t), G)[None]
    mask = np.where(np.arange(T)[None] <= np.arange(T)[:, None], 0, MASKED).astype(f)
    c = {
        "conv_w": rows(wt[:cut], wt[cut:], cols=2 * D),
        "wq": qkv[:, :, 0].reshape(D, -1), "wk": qkv[:, :, 1].reshape(D, -1), "wv": qkv[:, :, 2].reshape(D, -1),
        "wo": np.concatenate([pad_heads(w.T) for w in n["L0_ffn_Wo"]], 1),
        "w1": n["L0_ffn_W1"].transpose(2, 0, 1).reshape(D, -1),
        "w2": n["L0_ffn_W2"].reshape(E, D, FC, D).transpose(3, 0, 2, 1).reshape(D, -1),
        "mla_cat": np.concatenate([n["L0_attn_W_dq"], n["L0_attn_W_dkv"]], 1),
        "mla_uq": rows(n["L0_attn_W_uq"], cols=D),
        "mla_uk": rows(ukv[:, :D], cols=D), "mla_uv": rows(ukv[:, D:], cols=D),
        "mla_rope": rows(n["L0_attn_W_qr"], n["L0_attn_W_qr"][:, swap], n["L0_attn_W_kr"], n["L0_attn_W_kr"][:, swap],
                         cols=4 * ROPE),
        "mla_wo": pad_heads(n["L0_attn_W_o"].T),
        "gate_w": n["L0_ffn_gate_Wk"].T, "gate_q": n["L0_ffn_expert_queries"].T,
        "cols": rows(*[n[k][:, None] for k in ("L0_tok_b", "L0_tok_gamma", "L0_tok_beta", "L0_ffn_gate_bk", "L0_attn_q_ln_g",
                                               "L0_attn_q_ln_b", "L0_attn_kv_ln_g", "L0_attn_kv_ln_b")], cols=len(COLS)),
        "ecols": np.stack([bqkv[:, 0], bqkv[:, 1], *(bf1[:, i] for i in range(FC)), n["L0_ffn_bf2"], n["L0_ffn_g1"],
                           n["L0_ffn_be1"], bv[:, :, 0], bv[:, :, 1]]).reshape(-1, D).T,
        "bo_rows": np.broadcast_to(n["L0_ffn_bo"].reshape(1, -1), (128, E * D)),
        "g2_rows": np.broadcast_to(n["L0_ffn_g2"].reshape(1, -1), (128, E * D)),
        "be2": rows(n["L0_ffn_be2"], cols=D),
        "ident": np.eye(D, dtype=f),
        "causal": rows(mask, mask.T, cols=2 * T) if False else np.concatenate(
            [np.pad(mask, ((0, 128 - T), (0, 0))), np.pad(mask.T, ((0, 128 - T), (0, 0)))], 1),
        "rope_tab": rows(np.broadcast_to(cos, (ROPE, C)), sign * sin, cols=2 * C),
        "tri": np.broadcast_to(np.tril(np.ones((E, E), f), -1).reshape(1, -1), (128, E * E)),
    }
    return x.transpose(2, 0, 1), c


def kernel(**inputs):
    import concourse.bacc as bacc
    from concourse.bass_utils import run_bass_kernel_spmd

    named = {k: np.asarray(v) for k, v in inputs.items()}
    xw, consts = layouts(named.pop("x"), named)
    arrays = {f"in_{k}": np.ascontiguousarray(v) for k, v in {**consts, "x": xw}.items()}
    nc = bacc.Bacc("TRN2", target_bir_lowering=False, num_devices=1)
    aps = {k: nc.dram_tensor(k, v.shape, mybir.dt.from_np(v.dtype), kind="ExternalInput").ap() for k, v in arrays.items()}
    out = nc.dram_tensor("out", (B, T, D), F32, kind="ExternalOutput").ap()
    build_program(nc, {k: aps[f"in_{k}"] for k in consts}, aps["in_x"], out)
    return run_bass_kernel_spmd(nc, [arrays], core_ids=[0]).results[0]["out"]
```

```python
from contextlib import ExitStack

import concourse.bass as bass
import concourse.mybir as mybir
import numpy as np

ALU = mybir.AluOpType
ACT = mybir.ActivationFunctionType
AX = mybir.AxisListType
F32 = mybir.dt.float32
BF16 = mybir.dt.bfloat16

B, T_IN, D_IN, CTX = 128, 125, 40, 5
T = T_IN - CTX + 1
D = 128
H, DH = 8, 16
G = 4
NQ = B // G
C = G * T
E, F = 8, 512
FC = F // D
QP, KVP = D // 2, 2 * D // 3
CAT = QP + KVP
ROPE = D // 8
DR = ROPE // H
PAIRS = ((0, 0), (0, 1), (0, 2), (1, 0), (1, 1), (2, 0))
STACK = len(PAIRS) * DH
STACK_R = STACK + len(PAIRS) * DR
SHIFTS = (3, 2)
HP = 32
HG = 4
VW = H * D
UNITS = E + 1
STEPS = UNITS * G
EPS = 1e-5
MASKED = -1e30
EXP_LN_SET = 6
MLA_SCALE = float((DH + ROPE // H) ** -0.5)
EXP_SCALE = float(DH ** -0.5)
GATE_SCALE = float(D ** -0.5)

COLS = ("conv_b", "gamma", "beta", "gate_b", "q_g", "q_b", "kv_g", "kv_b", "zero")
ECOLS = ("bq", "bk", "bf1_0", "bf1_1", "bf1_2", "bf1_3", "bf2", "g1", "be1", "bv_0", "bv_1")

CONSTS = (
    ("conv_w", 2 * D), ("wq", E * D), ("wk", E * D), ("wv", E * D), ("wo", E * 2 * D),
    ("w1", E * F), ("w2", E * F), ("mla_cat", CAT), ("mla_uq", D), ("mla_uk", D), ("mla_uv", D),
    ("mla_rope", 4 * HP), ("mla_wo", 2 * D), ("gate_w", D), ("gate_q", E), ("cols", len(COLS)),
    ("ecols", len(ECOLS) * E), ("bo_rows", E * D), ("g2_rows", E * D), ("be2", D), ("ident", D),
    ("causal", 2 * T), ("rope_tab", 2 * C), ("tri", E * E),
)


def build_program(nc, args, x_dram, out):
    with ExitStack() as ctx:
        def sb(name, cols, dt=F32):
            return ctx.enter_context(nc.sbuf_tensor(name, [128, cols], dt))

        class Signal:
            all = []

            def __init__(self, name, per_group=1):
                self.sem = ctx.enter_context(nc.semaphore(name))
                self.n = per_group
                Signal.all.append(self)

            def at(self, q, k):
                return q * self.n + (self.n + k)

        sums, log_sums, recip = sb("sums", 2 * T), sb("log_sums", 2 * T), sb("recip", 2 * T)
        const = {name: recip if name == "causal" else sb(name, n) for name, n in CONSTS}
        c_ = const
        ident, tri, rope_tab = const["ident"], const["tri"], const["rope_tab"]
        col = {n: const["cols"][:, i:i + 1] for i, n in enumerate(COLS)}
        ident_b = sb("ident_b", D, BF16)
        causal_b = sb("causal_b", 2 * T, BF16)
        minus_half = sb("minus_half", 2 * G)

        x1T = sb("x1T", E * C)
        x_win = [[sb("x_win0", C), sb("x_win1", C)], [x1T[:, 0:C], x1T[:, C:2 * C]]]
        relu_x = [sb("relu_x", C), x1T[:, 2 * C:3 * C]]
        bn = sb("bn", 8)
        h_tok, x_tok, z_tok, s_tok, xbo = (sb(n, G * D) for n in ("h_tok", "x_tok", "z_tok", "s_tok", "xbo"))
        h1_tok, acc = sb("h1_tok", G * D), sb("acc", G * D)
        x0T, xT = sb("x0T", C), sb("xT", C)
        y2, yT = sb("y2", C), [sb("yT0", C), sb("yT1", C)]
        z_cat = sb("z_cat", G * CAT)
        q_part, k_part = ([[sb(f"{n}{i}{j}", C, BF16) for j in range(3)] for i in range(2)]
                          for n in ("q_part", "k_part"))
        q_left, k_left = sb("q_left", C), sb("k_left", C)
        q_stack, k_stack = ([sb(f"{n}{i}", H * C, BF16) for i in range(2)] for n in ("q_stack", "k_stack"))
        rotary, rotary_left = sb("rotary", C), sb("rotary_left", C)
        r_part = [sb(f"r_part{j}", C, BF16) for j in range(3)]
        conv_stats = q_left[:, 0:NQ * 6]
        v_one = [sb("v_one0", G * H * HP), sb("v_one1", G * H * HP)]
        probs = [sb("probs0", H * T), sb("probs1", H * T)]
        neg_max = [sb("neg_max0", H, BF16), sb("neg_max1", H, BF16)]
        h1T = sb("h1T", FC * C)
        st6, mv, veps, rstd = sb("st6", G * 6), sb("mv", G * 2), sb("veps", G), sb("rstd", G)
        a_st6, a_mv, a_veps, a_rstd = (
            sb(n, 2 * G * k) for n, k in (("a_st6", 6), ("a_mv", 2), ("a_veps", 1), ("a_rstd", 1)))
        g_max, g_sum, g_rec = sb("g_max", G), sb("g_sum", G), sb("g_rec", G)
        g_d, g_e, g_p, g_rank, g_mask = (sb(n, G * E) for n in ("g_d", "g_e", "g_p", "g_rank", "g_mask"))
        gated, rg = sb("gated", G * E), sb("rg", G)
        ctx_pad = [h1T[:, 0:2 * C], h1T[:, 2 * C:4 * C]]
        mla_ctx = sb("mla_ctx", 2 * C)
        w_tok = s_tok
        g_gt, g_ge = s_tok[:, 0:G * E * E], s_tok[:, G * E * E:2 * G * E * E]
        cqT, ckvT, h_bn = y2, yT[0], yT[1]
        keysT, gT = y2, x0T
        z0_tok = h1_tok
        rope_a, rope_b = h_bn, h1_tok[:, 0:C]

        psum = ctx.enter_context(nc.psum_tensor("psum", [128, 8, 512], F32))

        def signals(names, per_group=1):
            return [Signal(n, per_group) for n in names.split()]

        consts_in, zeroed, setup_dve, setup_pe, setup_rs = (
            ctx.enter_context(nc.semaphore(n)) for n in ("consts_in", "zeroed", "setup_dve", "setup_pe", "setup_rs"))
        s_conv, s_relu, s_bnst = (signals(f"{n}0 {n}1") for n in ("s_conv", "s_relu", "s_bnst"))
        s_win = signals("s_win0 s_win1", 16 * CTX)
        x_in, rotary_in = Signal("x_in", 16 * CTX), Signal("rotary_in", 2 * 16 * len(PAIRS))
        (conv_done, relu_done, hbn_done, hbnT_done, z0_done, z0T_done, x0T_done, cat_done, zcat_done, catT_done,
         catT_out, mla_v, rope_proj, rope_mul, rotary_done, r_top, r_rest, r_mid, r_low,
         h1_done, z1_done, z1T_done, xT_done) = signals(
            "conv_done relu_done hbn_done hbnT_done z0_done z0T_done x0T_done cat_done zcat_done catT_done "
            "catT_out mla_v rope_proj rope_mul rotary_done r_top r_rest r_mid r_low "
            "h1_done z1_done z1T_done xT_done")
        a_stats, a_aggr, a_veps_done, a_rstd_done = signals("a_stats a_aggr a_veps_done a_rstd_done", 3)
        (keys_done, keys_out, gscore_done, gd_done, ge_done, gated_done, gTT_done, gT_done, be2_done,
         acc_init) = signals("keys_done keys_out gscore_done gd_done ge_done gated_done gTT_done gT_done be2_done acc_init")
        gchain = Signal("gchain", 13)
        v_proj = Signal("v_proj", E)
        q_proj, k_proj, v_out, wo_done = signals("q_proj k_proj v_out wo_done", UNITS)
        q_top, q_rest, q_mid, q_low = signals("q_top q_rest q_mid q_low", UNITS)
        k_top, k_rest, k_mid, k_low = signals("k_top k_rest k_mid k_low", UNITS)
        stacking = 16 * len(PAIRS)
        q_in, k_in = ([Signal(f"{n}0", stacking * (1 + E // 2)), Signal(f"{n}1", stacking * (E // 2))]
                      for n in ("q_in", "k_in"))
        a_done, max_done, b_done, exp_done, av_done, sums_done, log_done, rec_done, norm_done = signals(
            "a_done max_done b_done exp_done av_done sums_done log_done rec_done norm_done", STEPS)
        (xbo_done, res_done, stats_done, aggr_done, veps_done, rstd_done, zs_done, zsT_done, x1T_done) = signals(
            "xbo_done res_done stats_done aggr_done veps_done rstd_done zs_done zsT_done x1T_done", E)
        up_done, gelu1_done = signals("up_done gelu1_done", E * FC)
        (down_done, gelu2_done, y_done, yT_done, stats2_done, aggr2_done, veps2_done, rstd2_done, rg_done, w_done,
         acc_done) = signals("down_done gelu2_done y_done yT_done stats2_done aggr2_done veps2_done rstd2_done "
                             "rg_done w_done acc_done", E)
        out_sent = Signal("out_sent", 16)

        def tok(tile, b, width=D):
            return tile[0:T, b * width:(b + 1) * width]

        def seq(tile, b, parts=128, base=0):
            return tile[0:parts, base + b * T:base + (b + 1) * T]

        def bank(i, parts=128, cols=C):
            return psum[0:parts, i, 0:cols]

        def bank_tok(i, b):
            return psum[0:T, i, b * D:(b + 1) * D]

        def ecol(name, e):
            i = ECOLS.index(name)
            return const["ecols"][:, i * E + e:i * E + e + 1]

        def wslice(name, e):
            return const[name][:, e * D:(e + 1) * D]


        def parity(unit):
            return 0 if unit == 0 else (unit - 1) % 2

        def stack_count(unit):
            return stacking * (1 if unit == 0 else (unit - 1) // 2 + 1 + (1 - parity(unit)))

        def head(stack, h, b, rows):
            return stack[0:rows, h * C + b * T:h * C + (b + 1) * T]

        def qk_bias(unit, side):
            return col["zero"] if unit == 0 else ecol(("bq", "bk")[side], unit - 1)

        def rows_of(unit):
            return STACK_R if unit == 0 else STACK

        def steps_before(unit):
            return {0: -G, 1: G, 2: 0}.get(unit, (unit - 1) * G)

        def step_list(q, ahead):
            steps = [(q, e + 1, b, (e + 1) * G + b) for e in range(E) for b in range(G)]
            if ahead:
                steps += [(q + 1, 0, b, b) for b in range(G)]
            return steps

        def all_turns(eng, first, turn):
            first()
            with eng.Fori(0, NQ - 1) as q:
                turn(q, True)
            turn(NQ - 1, False)

        block = ctx.enter_context(nc.Block())

        def load_windows(eng, q, tiles, sem):
            for i in range(CTX):
                j, r = (0, i) if i < SHIFTS[0] else (1, i - SHIFTS[0])
                dst = tiles[j][r * D_IN:(r + 1) * D_IN, :].rearrange("p (g t) -> p g t", g=G)
                eng.dma_start(dst, x_dram[:, bass.ds(q * G, G), i:i + T]).then_inc(sem, 16)

        @block.sync
        def _(sp):
            for name, n in CONSTS:
                sp.dma_start(const[name][:, :], args[name]).then_inc(consts_in, 16)
            with sp.Fori(0, NQ // 2) as i:
                for p in range(2):
                    sp.wait_ge(s_conv[p].sem, s_conv[p].at(i, 0))
                    load_windows(sp, 2 * i + p, x_win[p], s_win[p].sem)

            def stack_up(q, unit):
                par = parity(unit)
                sp.wait_ge(b_done.sem, b_done.at(q, steps_before(unit)))
                sp.nop(nofuse=True)
                for side, parts, stack, low, arrived in ((0, q_part, q_stack, q_low, q_in),
                                                         (1, k_part, k_stack, k_low, k_in)):
                    sp.wait_ge(low.sem, low.at(q, unit + 1))
                    sp.nop(nofuse=True)
                    for i, pair in enumerate(PAIRS):
                        sp.dma_start(stack[par][i * DH:(i + 1) * DH, :],
                                     parts[par][pair[side]][:, :]).then_inc(arrived[par].sem, 16)

            def windows(n):
                sp.wait_ge(conv_done.sem, conv_done.at(n, 0))
                sp.nop(nofuse=True)
                load_windows(sp, n, x_win[0], x_in.sem)

            def stack_rotary(n):
                sp.wait_ge(r_low.sem, r_low.at(n, 1))
                sp.nop(nofuse=True)
                sp.wait_ge(b_done.sem, b_done.at(n, -STEPS + G))
                sp.nop(nofuse=True)
                for side, stack in enumerate((q_stack[0], k_stack[0])):
                    for i, pair in enumerate(PAIRS):
                        sp.dma_start(stack[STACK + i * DR:STACK + (i + 1) * DR, :],
                                     r_part[pair[side]][side * HP:side * HP + ROPE, :]).then_inc(rotary_in.sem, 16)

            def first():
                sp.wait_ge(s_conv[0].sem, s_conv[0].at(NQ // 2, 0))
                sp.wait_ge(zeroed, 1)
                windows(0)
                stack_rotary(0)
                for unit in range(3):
                    stack_up(0, unit)

            def turn(q, ahead):
                if ahead:
                    windows(q + 1)
                for unit in range(3, UNITS):
                    stack_up(q, unit)
                if ahead:
                    stack_rotary(q + 1)
                    for unit in range(3):
                        stack_up(q + 1, unit)
                sp.wait_ge(acc_done.sem, acc_done.at(q, E))
                sp.dma_start(out[bass.ds(q * G, G), :, :].rearrange("g t d -> t g d"),
                             acc[0:T, :].rearrange("p (g d) -> p g d", g=G)).then_inc(out_sent.sem, 16)

            all_turns(sp, first, turn)
            sp.wait_ge(out_sent.sem, out_sent.at(NQ - 1, 16))

        @block.tensor
        def _(pe):
            def conv(tiles, dst):
                for j, s in enumerate(SHIFTS):
                    m = pe.matmul(dst, c_["conv_w"][0:s * D_IN, j * D:(j + 1) * D], tiles[j][0:s * D_IN, :],
                                  start=j == 0, stop=j == 1)
                return m

            pe.wait_ge(consts_in, 16 * len(CONSTS))
            for e in range(E):
                for g in range(2):
                    m = pe.matmul(psum[:, 2 + e // 4, (e % 4) * D:(e % 4 + 1) * D],
                                  ecol(f"bv_{g}", e).to_broadcast([128, 128]),
                                  const["wo"][:, (2 * e + g) * D:(2 * e + g + 1) * D], start=g == 0, stop=g == 1)
            m.then_inc(setup_pe, 1)
            with pe.Fori(0, NQ // 2) as i:
                for p in range(2):
                    pe.wait_ge(s_win[p].sem, s_win[p].at(i, 16 * CTX))
                    pe.wait_ge(s_relu[p].sem, s_relu[p].at(i, 0))
                    conv(x_win[p], bank(p)).then_inc(s_conv[p].sem, 1)

            def score_max(q, unit, b, step):
                par, mla, n = parity(unit), unit == 0, rows_of(unit)
                if b == 0:
                    pe.wait_ge(q_in[par].sem, q_in[par].at(q, stack_count(unit)))
                    pe.wait_ge(k_in[par].sem, k_in[par].at(q, stack_count(unit)))
                    if mla:
                        pe.wait_ge(rotary_in.sem, rotary_in.at(q, rotary_in.n))
                pe.wait_ge(max_done.sem, max_done.at(q, step))
                for h in range(H):
                    m = pe.matmul(psum[0:T, h // HG, (h % HG) * T:(h % HG + 1) * T], head(q_stack[par], h, b, n),
                                  head(k_stack[par], h, b, n), start=h % HG == 0 or not mla, stop=True,
                                  skip_group_check=True)
                if mla:
                    for half in range(2):
                        m = pe.matmul(psum[0:T, half, 0:C], ident_b[0:T, 0:T],
                                      causal_b[0:T, 0:T].rearrange("p (o k) -> p o k", o=1).to_broadcast([T, HG, T]),
                                      start=False, stop=True, skip_group_check=True)
                m.then_inc(a_done.sem, 1)

            def score_exp(q, unit, b, step):
                par, mla, n = parity(unit), unit == 0, rows_of(unit)
                pe.wait_ge(exp_done.sem, exp_done.at(q, step))
                for h in range(H):
                    pe.matmul(psum[0:T, 2 + h // HG, (h % HG) * T:(h % HG + 1) * T], head(k_stack[par], h, b, n),
                              head(q_stack[par], h, b, n), start=h % HG == 0, stop=True, skip_group_check=True)
                if mla:
                    for half in range(2):
                        pe.matmul(psum[0:T, 2 + half, 0:C], ident_b[0:T, 0:T],
                                  causal_b[0:T, T:2 * T].rearrange("p (o k) -> p o k", o=1).to_broadcast([T, HG, T]),
                                  start=False, stop=True, skip_group_check=True)
                pe.wait_ge(max_done.sem, max_done.at(q, step + 1))
                for h in range(H):
                    m = pe.matmul(psum[0:T, 2 + h // HG, (h % HG) * T:(h % HG + 1) * T],
                                  neg_max[b % 2][0:T, h:h + 1].to_broadcast([T, T]), ident_b[0:T, 0:T],
                                  start=False, stop=True, skip_group_check=True)
                m.then_inc(b_done.sem, 1)

            def weigh(q, unit, b, step):
                par = parity(unit)
                if b == 0:
                    pe.wait_ge(v_out.sem, v_out.at(q, unit + 1))
                pe.wait_ge(exp_done.sem, exp_done.at(q, step + 1))
                pe.wait_ge(norm_done.sem, norm_done.at(q, step))
                pe.nop(nofuse=True)
                for h in range(H):
                    g, j = h // HG, h % HG
                    m = pe.matmul(psum[HP * j:HP * (j + 1), 7, g * T:(g + 1) * T],
                                  v_one[par][0:T, (b * H + h) * HP:(b * H + h + 1) * HP],
                                  probs[b % 2][0:T, h * T:(h + 1) * T], start=True, stop=True, skip_group_check=True)
                m.then_inc(av_done.sem, 1)

            def out_proj(q, unit, src, w, e, i):
                pe.wait_ge(norm_done.sem, norm_done.at(q, (unit + 1) * G))
                for b in range(G):
                    for g in range(2):
                        m = pe.matmul(bank_tok(i, b), src[:, g * C + b * T:g * C + (b + 1) * T],
                                      const[w][:, (2 * e + g) * D:(2 * e + g + 1) * D], start=g == 0, stop=g == 1)
                m.then_inc(wo_done.sem, 1)

            def to_feature(src, i, signal, parts=D, base=0, width=D):
                for b in range(G):
                    m = pe.transpose(psum[0:parts, i, b * T:(b + 1) * T],
                                     src[0:T, b * width + base:b * width + base + parts], ident[0:T, 0:T])
                if signal is not None:
                    m.then_inc(signal.sem, 1)

            def to_token(src, i, signal):
                for b in range(G):
                    m = pe.transpose(bank_tok(i, b), seq(src, b), ident[:, :])
                m.then_inc(signal.sem, 1)

            def project(w, src, i, signal, k=D, m=D, off=0):
                ins = pe.matmul(bank(i, m), w[0:k, off:off + m], src[0:k, :], start=True, stop=True)
                if signal is not None:
                    ins.then_inc(signal.sem, 1)

            def proj_q(q, e, i):
                project(wslice("wq", e), xT, i, q_proj)

            def proj_k(q, e, i):
                project(wslice("wk", e), xT, i, k_proj)

            def proj_v(q, e, i):
                for b in range(G):
                    m = pe.matmul(bank_tok(i, b), seq(xT, b), wslice("wv", e), start=True, stop=True)
                m.then_inc(v_proj.sem, 1)

            def a_conv(n):
                pe.wait_ge(x_in.sem, x_in.at(n, 16 * CTX))
                conv(x_win[0], bank(4)).then_inc(conv_done.sem, 1)

            def a_hbn(n):
                pe.wait_ge(hbn_done.sem, hbn_done.at(n, 1))
                to_token(h_bn, 6, hbnT_done)

            def a_z0(n):
                pe.wait_ge(z0_done.sem, z0_done.at(n, 1))
                to_feature(z0_tok, 6, z0T_done)

            def a_cat(n):
                pe.wait_ge(x0T_done.sem, x0T_done.at(n, 1))
                for b in range(G):
                    m = pe.matmul(psum[0:T, 6 - 2 * (b // 2), (b % 2) * CAT:(b % 2 + 1) * CAT], seq(x0T, b),
                                  c_["mla_cat"][:, :], start=True, stop=True)
                m.then_inc(cat_done.sem, 1)

            def a_catT(n):
                pe.wait_ge(zcat_done.sem, zcat_done.at(n, 1))
                pe.nop(nofuse=True)
                to_feature(z_cat, 6, None, QP, 0, CAT)
                to_feature(z_cat, 4, catT_done, KVP, QP, CAT)

            def a_rope(n):
                pe.wait_ge(catT_out.sem, catT_out.at(n, 1))
                pe.nop(nofuse=True)
                for k, src, rows in ((0, cqT, QP), (1, x0T, D)):
                    for i in range(2):
                        m = pe.matmul(psum[HP * k:HP * (k + 1), 6 - 2 * i, 0:C],
                                      c_["mla_rope"][0:rows, (2 * k + i) * HP:(2 * k + i + 1) * HP], src[0:rows, :],
                                      start=True, stop=True, skip_group_check=True)
                m.then_inc(rope_proj.sem, 1)

            def a_qk(n):
                project(c_["mla_uq"], cqT, 4, q_proj, k=QP)
                project(c_["mla_uk"], ckvT, 5, k_proj, k=KVP)

            def a_v(n):
                pe.wait_ge(q_rest.sem, q_rest.at(n, 1))
                for b in range(G):
                    m = pe.matmul(bank_tok(4, b), seq(ckvT, b, KVP), c_["mla_uv"][0:KVP, :], start=True, stop=True)
                m.then_inc(mla_v.sem, 1)

            def a_xT(n, i):
                pe.wait_ge(z1_done.sem, z1_done.at(n, 1))
                to_feature(x_tok, i, z1T_done)

            def first():
                a_conv(0)
                a_hbn(0)
                a_z0(0)
                a_cat(0)
                a_catT(0)
                a_rope(0)
                pe.wait_ge(rotary_done.sem, rotary_done.at(0, 1))
                a_qk(0)
                a_v(0)
                score_max(0, 0, 0, 0)
                for b in range(G):
                    if b + 1 < G:
                        score_max(0, 0, b + 1, b + 1)
                    score_exp(0, 0, b, b)
                    if b:
                        weigh(0, 0, b - 1, b - 1)
                weigh(0, 0, G - 1, G - 1)
                out_proj(0, 0, mla_ctx, "mla_wo", 0, 6)
                a_xT(0, 5)
                pe.wait_ge(xT_done.sem, xT_done.at(0, 1))
                proj_q(0, 0, 6)
                proj_k(0, 0, 7)
                proj_v(0, 0, 5)
                proj_q(0, 1, 4)
                pe.wait_ge(q_rest.sem, q_rest.at(0, 2))
                proj_k(0, 1, 6)

            def turn(q, ahead):
                n = q + 1
                steps = step_list(q, ahead)

                def more(e, b):
                    if b == 0 and e < E - 1:
                        pe.wait_ge(v_out.sem, v_out.at(q, e + 2))
                        if e > 0:
                            pe.wait_ge(x1T_done.sem, x1T_done.at(q, e - 1))
                        if ahead and e in (1, 4, 5, 6):
                            reader = {1: relu_done, 4: zcat_done, 5: catT_out, 6: rotary_done}[e]
                            pe.wait_ge(reader.sem, reader.at(n, 1))
                        if e + 2 < E:
                            proj_q(q, e + 2, 4)
                            proj_k(q, e + 2, 5)
                        elif ahead:
                            a_qk(n)
                    if e == 0:
                        if b == 0:
                            project(c_["gate_w"], xT, 6, keys_done)
                        if b == 1:
                            pe.wait_ge(keys_out.sem, keys_out.at(q, 1))
                            for i in range(G):
                                m = pe.matmul(psum[0:T, 6, i * E:(i + 1) * E], seq(keysT, i), c_["gate_q"][:, :],
                                              start=True, stop=True)
                            m.then_inc(gscore_done.sem, 1)
                        if b == 3:
                            pe.wait_ge(gated_done.sem, gated_done.at(q, 1))
                            pe.nop(nofuse=True)
                            for i in range(G):
                                m = pe.transpose(psum[0:E, 6, i * T:(i + 1) * T], gated[0:T, i * E:(i + 1) * E],
                                                 ident[0:T, 0:T])
                            m.then_inc(gTT_done.sem, 1)
                    if e == 1 and b == 0:
                        pe.wait_ge(gT_done.sem, gT_done.at(q, 1))
                        for i in range(G):
                            m = pe.matmul(bank_tok(6, i), seq(gT, i, E), c_["be2"][0:E, :], start=True, stop=True)
                        m.then_inc(be2_done.sem, 1)
                    if b == 1 and e > 0:
                        if e == 1:
                            pe.wait_ge(acc_init.sem, acc_init.at(q, 1))
                        elif ahead and e < E:
                            reader = {2: z0_done, 3: x0T_done, 4: zcat_done, 5: catT_out, 6: rotary_done,
                                      7: rotary_done}[e]
                            pe.wait_ge(reader.sem, reader.at(n, 1))
                        else:
                            pe.wait_ge(res_done.sem, res_done.at(q, e - 1))
                        if e == 7:
                            pe.wait_ge(res_done.sem, res_done.at(q, 6))
                        out_proj(q, e, ctx_pad[(e - 1) % 2], "wo", e - 1, 6)
                    if b == 1 and e + 1 < E:
                        if e + 2 < E:
                            pe.wait_ge(q_rest.sem, q_rest.at(q, e + 4))
                        elif ahead:
                            pe.wait_ge(q_rest.sem, q_rest.at(n, 1))
                        proj_v(q, e + 1, 4)
                    if b == 3 and e > 0:
                        pe.wait_ge(zs_done.sem, zs_done.at(q, e))
                        if e + 2 < E:
                            pe.wait_ge(k_rest.sem, k_rest.at(q, e + 4))
                        elif ahead:
                            pe.wait_ge(k_rest.sem, k_rest.at(n, 1))
                        pe.wait_ge(x1T_done.sem, x1T_done.at(q, e - 1))
                        to_feature(z_tok, 5, zsT_done)
                    if ahead:
                        if (e, b) == (0, 2):
                            pe.wait_ge(v_out.sem, v_out.at(q, 3))
                            a_conv(n)
                        if b == 2 and 0 < e < 6:
                            pe.wait_ge(res_done.sem, res_done.at(q, e))
                            pe.wait_ge(v_out.sem, v_out.at(q, e + 3))
                            (None, a_hbn, a_z0, a_cat, a_catT, a_rope)[e](n)
                        if (e, b) == (E - 1, 1):
                            pe.wait_ge(v_out.sem, v_out.at(q, E + 1))
                            a_v(n)

                score_max(*steps[0])
                for i, (qq, unit, b, step) in enumerate(steps):
                    if i + 1 < len(steps):
                        score_max(*steps[i + 1])
                    score_exp(qq, unit, b, step)
                    if i:
                        weigh(*steps[i - 1])
                    more(unit - 1 if unit else E, b)
                weigh(*steps[-1])
                if not ahead:
                    more(E, 1)
                    more(E, 3)

                def up(e, c):
                    pe.matmul(bank(c), const["w1"][:, e * F + c * D:e * F + (c + 1) * D], x1T[:, e * C:(e + 1) * C],
                              start=True, stop=True).then_inc(up_done.sem, 1)

                def tail(e):
                    pe.wait_ge(y_done.sem, y_done.at(q, e + 1))
                    if e:
                        pe.wait_ge(w_done.sem, w_done.at(q, e - 1))
                    if ahead and e != 1:
                        reader, k = {0: (h1_done, 1), 2: (xT_done, 1), 3: (q_rest, 2), 4: (k_rest, 2), 5: (q_rest, 3),
                                     6: (k_rest, 3), 7: (v_out, 2)}[e]
                        pe.wait_ge(reader.sem, reader.at(n, k))
                    to_token(yT[e % 2], 7 - e % 2, yT_done)

                def behind(e):
                    i = 7 - e % 2
                    if e >= 2:
                        pe.wait_ge(w_done.sem, w_done.at(q, e - 1))
                    if e == 0:
                        out_proj(n, 0, mla_ctx, "mla_wo", 0, i)
                    elif e == 2:
                        a_xT(n, i)
                    elif e == 3:
                        pe.wait_ge(xT_done.sem, xT_done.at(n, 1))
                        proj_q(n, 0, i)
                    elif e == 4:
                        proj_k(n, 0, i)
                    elif e == 5:
                        proj_q(n, 1, i)
                    elif e == 6:
                        proj_k(n, 1, i)
                    elif e == 7:
                        proj_v(n, 0, i)

                pe.wait_ge(x1T_done.sem, x1T_done.at(q, 1))
                pe.wait_ge(max_done.sem, max_done.at(n if ahead else q, G if ahead else STEPS))
                pe.wait_ge(exp_done.sem, exp_done.at(n if ahead else q, G if ahead else STEPS))
                for c in range(FC):
                    up(0, c)
                pe.wait_ge(x1T_done.sem, x1T_done.at(q, E))
                if ahead:
                    pe.wait_ge(v_out.sem, v_out.at(n, 1))
                for e in range(E):
                    for c in range(FC):
                        pe.wait_ge(gelu1_done.sem, gelu1_done.at(q, e * FC + c + 1))
                        if c == 0 and e:
                            pe.wait_ge(gelu2_done.sem, gelu2_done.at(q, e - 1))
                        m = pe.matmul(bank(4 + e % 2), const["w2"][:, e * F + c * D:e * F + (c + 1) * D],
                                      h1T[:, c * C:(c + 1) * C], start=c == 0, stop=c == FC - 1)
                        if c == FC - 1:
                            m.then_inc(down_done.sem, 1)
                        if e + 1 < E:
                            up(e + 1, c)
                        if c == 1 and e:
                            tail(e - 1)
                    if ahead:
                        behind(e)
                tail(E - 1)

            all_turns(pe, first, turn)

        @block.scalar
        def _(act):
            def exp_log_table():
                act.add_instruction(mybir.InstLoadActFuncSet(
                    act_func_set_id=EXP_LN_SET, name=nc.get_next_instruction_name(), engine=act.engine))

            act.wait_ge(consts_in, 16 * len(CONSTS))
            with act.Fori(0, NQ // 2) as i:
                for p in range(2):
                    act.wait_ge(s_conv[p].sem, s_conv[p].at(i, 1))
                    act.wait_ge(s_bnst[p].sem, s_bnst[p].at(i, 0))
                    act.activation(relu_x[p][:, :], bank(p), ACT.Relu, bias=col["conv_b"]).then_inc(s_relu[p].sem, 1)

            def exps(q, unit, b, step):
                act.wait_ge(b_done.sem, b_done.at(q, step + 1))
                act.wait_ge(av_done.sem, av_done.at(q, step - 1))
                act.activation(probs[b % 2][0:T, :].rearrange("p (a c) -> p a c", a=2), psum[0:T, 2:4, 0:C], ACT.Exp,
                               scale=MLA_SCALE if unit == 0 else EXP_SCALE).then_inc(exp_done.sem, 1)

            def reciprocals(q, unit, b, step):
                act.wait_ge(sums_done.sem, sums_done.at(q, step + 1))
                act.activation(log_sums[:, :], sums[:, :], ACT.Ln).then_inc(log_done.sem, 1)
                act.wait_ge(log_done.sem, log_done.at(q, step + 1))
                act.wait_ge(norm_done.sem, norm_done.at(q, step))
                act.activation(recip[:, :], log_sums[:, :], ACT.Exp, scale=-1.0).then_inc(rec_done.sem, 1)

            def top(q, unit, side, i):
                par = parity(unit)
                proj, done, parts, arrived = ((q_proj, q_top, q_part, q_in), (k_proj, k_top, k_part, k_in))[side]
                act.wait_ge(proj.sem, proj.at(q, unit + 1))
                act.wait_ge(arrived[par].sem, arrived[par].at(q, stack_count(unit) - stacking))
                act.activation(parts[par][0][:, :], bank(i), ACT.Identity,
                               bias=qk_bias(unit, side)).then_inc(done.sem, 1)

            def mid(q, unit, side):
                rest, done, parts, left = ((q_rest, q_mid, q_part, q_left), (k_rest, k_mid, k_part, k_left))[side]
                act.wait_ge(rest.sem, rest.at(q, unit + 1))
                act.activation(parts[parity(unit)][1][:, :], left[:, :], ACT.Copy).then_inc(done.sem, 1)

            def r_tops(n):
                act.wait_ge(rotary_done.sem, rotary_done.at(n, 1))
                act.wait_ge(rotary_in.sem, rotary_in.at(n, 0))
                act.activation(r_part[0][0:2 * HP, :], rotary[0:2 * HP, :], ACT.Copy).then_inc(r_top.sem, 1)

            def r_mids(n):
                act.wait_ge(r_rest.sem, r_rest.at(n, 1))
                act.activation(r_part[1][0:2 * HP, :], rotary_left[0:2 * HP, :], ACT.Copy).then_inc(r_mid.sem, 1)

            def v_copy(par, i):
                act.activation(v_one[par][0:T, :].rearrange("p (c x) -> p c x", x=HP)[:, :, 0:DH],
                               psum[0:T, i, :].rearrange("p (c x) -> p c x", x=DH), ACT.Copy).then_inc(v_out.sem, 1)

            def v_evac(q, e, i):
                act.wait_ge(v_proj.sem, v_proj.at(q, e + 1))
                act.wait_ge(av_done.sem, av_done.at(q, steps_before(e + 1)))
                v_copy(e % 2, i)

            def a_relu(n):
                act.wait_ge(conv_done.sem, conv_done.at(n, 1))
                act.wait_ge(hbn_done.sem, hbn_done.at(n, 0))
                act.activation(relu_x[0][:, :], bank(4), ACT.Relu, bias=col["conv_b"]).then_inc(relu_done.sem, 1)

            def a_x0T(n):
                act.wait_ge(z0T_done.sem, z0T_done.at(n, 1))
                act.activation(x0T[:, :], bank(6), ACT.Copy).then_inc(x0T_done.sem, 1)

            def a_latents(n):
                act.wait_ge(catT_done.sem, catT_done.at(n, 1))
                act.activation(cqT[0:QP, :], bank(6, QP), ACT.Identity, bias=col["q_b"][0:QP], scale=col["q_g"][0:QP])
                act.activation(ckvT[0:KVP, :], bank(4, KVP), ACT.Identity, bias=col["kv_b"][0:KVP],
                               scale=col["kv_g"][0:KVP]).then_inc(catT_out.sem, 1)

            def a_v_out(n):
                act.wait_ge(mla_v.sem, mla_v.at(n, 1))
                act.wait_ge(av_done.sem, av_done.at(n, steps_before(0)))
                v_copy(0, 4)

            def a_xT_out(n, i):
                act.wait_ge(z1T_done.sem, z1T_done.at(n, 1))
                act.activation(xT[:, :], bank(i), ACT.Copy).then_inc(xT_done.sem, 1)

            def first():
                for p in range(2):
                    act.wait_ge(s_bnst[p].sem, s_bnst[p].at(NQ // 2, 0))
                act.wait_ge(zeroed, 1)
                exp_log_table()
                a_relu(0)
                a_x0T(0)
                a_latents(0)
                r_tops(0)
                r_mids(0)
                top(0, 0, 0, 4)
                top(0, 0, 1, 5)
                mid(0, 0, 0)
                mid(0, 0, 1)
                a_v_out(0)
                for b in range(G):
                    exps(0, 0, b, b)
                    if b:
                        reciprocals(0, 0, b - 1, b - 1)
                reciprocals(0, 0, G - 1, G - 1)
                a_xT_out(0, 5)
                top(0, 1, 0, 6)
                top(0, 1, 1, 7)
                v_evac(0, 0, 5)
                mid(0, 1, 0)
                mid(0, 1, 1)
                top(0, 2, 0, 4)
                mid(0, 2, 0)
                top(0, 2, 1, 6)
                mid(0, 2, 1)

            def turn(q, ahead):
                n = q + 1
                steps = step_list(q, ahead)

                def x1_out(e):
                    act.wait_ge(zsT_done.sem, zsT_done.at(q, e + 1))
                    act.activation(x1T[:, e * C:(e + 1) * C], bank(5), ACT.Identity, bias=ecol("be1", e),
                                   scale=ecol("g1", e)).then_inc(x1T_done.sem, 1)

                def more(e, b):
                    after = (q, e + 3) if e + 2 < E else (n, 0)
                    if e + 2 < E or ahead and e + 2 == E:
                        if b == 0:
                            top(*after, 0, 4)
                            top(*after, 1, 5)
                        if b == 1:
                            mid(*after, 0)
                        if b == 2:
                            mid(*after, 1)
                    if b == 1 and e + 1 < E:
                        v_evac(q, e + 1, 4)
                    if (e, b) == (0, 0):
                        act.wait_ge(keys_done.sem, keys_done.at(q, 1))
                        act.activation(keysT[:, :], bank(6), ACT.Identity, bias=col["gate_b"]).then_inc(keys_out.sem, 1)
                    if (e, b) == (0, 2):
                        act.wait_ge(gd_done.sem, gd_done.at(q, 1))
                        act.activation(g_e[0:T, :], g_d[0:T, :], ACT.Exp, scale=GATE_SCALE).then_inc(ge_done.sem, 1)
                    if (e, b) == (0, 3):
                        act.wait_ge(gTT_done.sem, gTT_done.at(q, 1))
                        act.activation(gT[0:E, :], bank(6, E), ACT.Copy).then_inc(gT_done.sem, 1)
                    if b == 3 and e > 0:
                        x1_out(e - 1)
                    if ahead and b == 3 and e < E:
                        {0: a_relu, 2: a_x0T, 4: a_latents}.get(e, lambda n: None)(n)
                    if ahead and (e, b) == (5, 3):
                        r_tops(n)
                    if ahead and (e, b) == (6, 0):
                        r_mids(n)
                    if ahead and (e, b) == (E - 1, 1):
                        a_v_out(n)

                exp_log_table()
                for i, (qq, unit, b, step) in enumerate(steps):
                    exps(qq, unit, b, step)
                    if i:
                        reciprocals(*steps[i - 1])
                    more(unit - 1 if unit else E, b)
                reciprocals(*steps[-1])
                if not ahead:
                    x1_out(E - 1)

                def gelu1(e, c):
                    act.wait_ge(up_done.sem, up_done.at(q, e * FC + c + 1))
                    if e == 0:
                        act.wait_ge(wo_done.sem, wo_done.at(q, UNITS))
                    act.activation(h1T[:, c * C:(c + 1) * C], bank(c), ACT.Gelu,
                                   bias=ecol(f"bf1_{c}", e)).then_inc(gelu1_done.sem, 1)

                for c in range(FC):
                    gelu1(0, c)
                for e in range(E):
                    for c in range(FC):
                        if c == FC - 1:
                            act.wait_ge(down_done.sem, down_done.at(q, e + 1))
                            act.wait_ge(y_done.sem, y_done.at(q, e))
                            act.activation(y2[:, :], bank(4 + e % 2), ACT.Gelu, bias=ecol("bf2", e)).then_inc(gelu2_done.sem, 1)
                        if e + 1 < E:
                            gelu1(e + 1, c)
                    if ahead:
                        i = 7 - e % 2
                        if e == 2:
                            a_xT_out(n, i)
                        if 3 < e:
                            mid(n, *((1, 0), (1, 1), (2, 0), (2, 1))[e - 4])
                        if 3 <= e < 7:
                            top(n, *((1, 0), (1, 1), (2, 0), (2, 1))[e - 3], i)
                        if e == 7:
                            v_evac(n, 0, i)

            all_turns(act, first, turn)

        @block.vector
        def _(dve):
            for t_ in v_one:
                dve.memset(t_[:, :], 1.0)
            dve.memset(minus_half[:, :], -0.5).then_inc(zeroed, 1)
            dve.wait_ge(consts_in, 16 * len(CONSTS))
            dve.tensor_copy(ident_b[:, :], ident[:, :])
            dve.tensor_copy(causal_b[:, :], const["causal"][:, :])
            dve.wait_ge(setup_pe, 1)
            for i in range(2):
                half = const["bo_rows"][:, i * 4 * D:(i + 1) * 4 * D]
                m = dve.tensor_tensor(half, psum[:, 2 + i, :], half, ALU.add)
            m.then_inc(setup_dve, 1)
            with dve.Fori(0, NQ // 2) as i:
                for p in range(2):
                    dve.wait_ge(s_relu[p].sem, s_relu[p].at(i, 1))
                    dve.bn_stats(conv_stats[:, bass.ds((2 * i + p) * 6, 6)], relu_x[p][:, :]).then_inc(s_bnst[p].sem, 1)
            for p in range(2):
                dve.wait_ge(s_bnst[p].sem, s_bnst[p].at(NQ // 2, 0))
            dve.bn_aggr(bn[:, 0:2], conv_stats[:, :]).then_inc(setup_dve, 1)
            dve.wait_ge(setup_dve, 2)
            dve.tensor_scalar(bn[:, 2:3], bn[:, 1:2], EPS, None, ALU.add).then_inc(setup_dve, 1)
            dve.wait_ge(setup_rs, 1)
            dve.tensor_scalar(bn[:, 4:5], bn[:, 3:4], col["gamma"], None, ALU.mult).then_inc(setup_dve, 1)
            dve.wait_ge(setup_dve, 4)
            dve.tensor_scalar(bn[:, 5:6], bn[:, 0:1], bn[:, 4:5], None, ALU.mult).then_inc(setup_dve, 1)
            dve.wait_ge(setup_dve, 5)
            dve.tensor_tensor(bn[:, 6:7], col["beta"], bn[:, 5:6], ALU.subtract).then_inc(setup_dve, 1)
            dve.wait_ge(setup_dve, 6)

            def norm_stats(q, k, sources, tiles, sigs):
                t_st, t_mv, t_veps = tiles
                s_stats, s_aggr, s_veps, s_rstd = sigs
                m = len(sources)
                for i, src in enumerate(sources):
                    ins = dve.bn_stats(t_st[0:T, 6 * i:6 * i + 6], src)
                ins.then_inc(s_stats.sem, 1)
                dve.wait_ge(s_stats.sem, s_stats.at(q, k))
                dve.nop(nofuse=True)
                for i in range(m):
                    ins = dve.bn_aggr(t_mv[0:T, 2 * i:2 * i + 2], t_st[0:T, 6 * i:6 * i + 6])
                ins.then_inc(s_aggr.sem, 1)
                dve.wait_ge(s_aggr.sem, s_aggr.at(q, k))
                dve.wait_ge(s_rstd.sem, s_rstd.at(q, k - 1))
                dve.tensor_scalar(t_veps[0:T, 0:m], t_mv[0:T, 1:2 * m:2], EPS, None, ALU.add).then_inc(s_veps.sem, 1)

            def standardize(pairs, t_mv, t_rstd):
                for i, (dst, src) in enumerate(pairs):
                    ins = dve.tensor_scalar(dst, src, t_mv[0:T, 2 * i:2 * i + 1], t_rstd[0:T, i:i + 1],
                                            ALU.subtract, ALU.mult)
                return ins

            ahead_tiles, ahead_sigs = (a_st6, a_mv, a_veps), (a_stats, a_aggr, a_veps_done, a_rstd_done)
            tiles = (st6, mv, veps)

            def row_max(q, unit, b, step):
                dve.wait_ge(a_done.sem, a_done.at(q, step + 1))
                dve.wait_ge(b_done.sem, b_done.at(q, step - 1))
                dve.tensor_reduce(neg_max[b % 2][0:T, :].rearrange("p (a h) -> p a h", a=2),
                                  psum[0:T, 0:2, 0:C].rearrange("p a (h k) -> p a h k", h=HG),
                                  AX.X, ALU.max, negate=True).then_inc(max_done.sem, 1)

            def spread_sums(q, unit, b, step):
                dve.wait_ge(av_done.sem, av_done.at(q, step + 1))
                dve.wait_ge(log_done.sem, log_done.at(q, step))
                dve.nop(nofuse=True)
                dve.stream_shuffle(sums[:, :], psum[:, 7, 0:2 * T], [DH] * HP).then_inc(sums_done.sem, 1)

            def norm_ctx(q, unit, b, step):
                dst = mla_ctx if unit == 0 else ctx_pad[(unit - 1) % 2]
                dve.wait_ge(rec_done.sem, rec_done.at(q, step + 1))
                if unit >= 3:
                    dve.wait_ge(wo_done.sem, wo_done.at(q, unit - 1))
                dve.tensor_tensor(dst[:, :].rearrange("p (g c) -> p g c", g=2)[:, :, b * T:(b + 1) * T],
                                  psum[:, 7, 0:2 * T].rearrange("p (g t) -> p g t", g=2),
                                  recip[:, :].rearrange("p (g t) -> p g t", g=2), ALU.mult).then_inc(norm_done.sem, 1)

            def a_hbn(n):
                dve.wait_ge(relu_done.sem, relu_done.at(n, 1))
                dve.tensor_scalar(h_bn[:, :], relu_x[0][:, :], bn[:, 4:5], bn[:, 6:7], ALU.mult,
                                  ALU.add).then_inc(hbn_done.sem, 1)

            def a_norm0(n):
                dve.wait_ge(hbnT_done.sem, hbnT_done.at(n, 1))
                norm_stats(n, 1, [bank_tok(6, b) for b in range(G)], ahead_tiles, ahead_sigs)
                dve.tensor_copy(h_tok[0:T, :], psum[0:T, 6, :])

            def a_norm0_out(n):
                dve.wait_ge(a_rstd_done.sem, a_rstd_done.at(n, 1))
                standardize([(tok(z0_tok, b), bank_tok(6, b)) for b in range(G)], a_mv, a_rstd).then_inc(z0_done.sem, 1)

            cat_pairs = [(z_cat[0:T, b * CAT + o:b * CAT + o + w],
                          psum[0:T, 6 - 2 * (b // 2), (b % 2) * CAT + o:(b % 2) * CAT + o + w])
                         for b in range(G) for o, w in ((0, QP), (QP, KVP))]

            def a_norm1(n):
                dve.wait_ge(cat_done.sem, cat_done.at(n, 1))
                norm_stats(n, 2, [p[1] for p in cat_pairs], ahead_tiles, ahead_sigs)

            def a_norm1_out(n):
                dve.wait_ge(a_rstd_done.sem, a_rstd_done.at(n, 2))
                standardize(cat_pairs, a_mv, a_rstd).then_inc(zcat_done.sem, 1)

            def a_rotate(n):
                k = 2 * HP
                dve.wait_ge(rope_proj.sem, rope_proj.at(n, 1))
                dve.wait_ge(r_rest.sem, r_rest.at(n, 0))
                dve.tensor_tensor(rope_a[0:k, :], bank(6, k), rope_tab[0:k, 0:C], ALU.mult)
                dve.tensor_tensor(rope_b[0:k, :], bank(4, k), rope_tab[0:k, C:2 * C], ALU.mult).then_inc(rope_mul.sem, 1)
                dve.wait_ge(rope_mul.sem, rope_mul.at(n, 1))
                dve.tensor_tensor(rotary[0:k, :], rope_a[0:k, :], rope_b[0:k, :], ALU.add).then_inc(rotary_done.sem, 1)

            def a_r_rest(n):
                dve.wait_ge(r_top.sem, r_top.at(n, 1))
                dve.wait_ge(r_low.sem, r_low.at(n, 0))
                dve.tensor_tensor(rotary_left[0:2 * HP, :], rotary[0:2 * HP, :], r_part[0][0:2 * HP, :],
                                  ALU.subtract).then_inc(r_rest.sem, 1)

            def rest(q, unit, side, i):
                top_, done, low, parts, left = ((q_top, q_rest, q_low, q_part, q_left),
                                                (k_top, k_rest, k_low, k_part, k_left))[side]
                dve.wait_ge(top_.sem, top_.at(q, unit + 1))
                dve.wait_ge(low.sem, low.at(q, unit))
                dve.scalar_tensor_tensor(left[:, :], bank(i), qk_bias(unit, side), parts[parity(unit)][0][:, :],
                                         ALU.add, ALU.subtract).then_inc(done.sem, 1)

            def a_norm2(n, i):
                dve.wait_ge(wo_done.sem, wo_done.at(n, 1))
                dve.tensor_tensor(h1_tok[0:T, :], psum[0:T, i, :], h_tok[0:T, :], ALU.add).then_inc(h1_done.sem, 1)
                dve.wait_ge(h1_done.sem, h1_done.at(n, 1))
                norm_stats(n, 3, [tok(h1_tok, b) for b in range(G)], ahead_tiles, ahead_sigs)

            def a_norm2_out(n):
                dve.wait_ge(a_rstd_done.sem, a_rstd_done.at(n, 3))
                standardize([(tok(x_tok, b), tok(h1_tok, b)) for b in range(G)], a_mv, a_rstd).then_inc(z1_done.sem, 1)

            def first():
                a_hbn(0)
                a_norm0(0)
                a_norm0_out(0)
                a_norm1(0)
                a_norm1_out(0)
                a_rotate(0)
                a_r_rest(0)
                rest(0, 0, 0, 4)
                rest(0, 0, 1, 5)
                row_max(0, 0, 0, 0)
                for b in range(G):
                    if b > 1:
                        norm_ctx(0, 0, b - 2, b - 2)
                    if b + 1 < G:
                        row_max(0, 0, b + 1, b + 1)
                    if b:
                        spread_sums(0, 0, b - 1, b - 1)
                norm_ctx(0, 0, G - 2, G - 2)
                spread_sums(0, 0, G - 1, G - 1)
                norm_ctx(0, 0, G - 1, G - 1)
                a_norm2(0, 6)
                a_norm2_out(0)
                rest(0, 1, 0, 6)
                rest(0, 1, 1, 7)
                rest(0, 2, 0, 4)
                rest(0, 2, 1, 6)

            def turn(q, ahead):
                n = q + 1
                steps = step_list(q, ahead)
                count = [0]

                def link(ins):
                    count[0] += 1
                    ins.then_inc(gchain.sem, 1)
                    dve.wait_ge(gchain.sem, gchain.at(q, count[0]))

                v3 = lambda t_: t_[0:T, :].rearrange("p (b e) -> p b e", b=G)
                v4 = lambda t_: t_[0:T, :].rearrange("p (b e j) -> p b e j", b=G, e=E)
                per_tok = lambda t_: t_[0:T, :].rearrange("p (b o) -> p b o", o=1).to_broadcast([T, G, E])

                def gate_scores():
                    dve.wait_ge(gscore_done.sem, gscore_done.at(q, 1))
                    sc = psum[0:T, 6, 0:G * E].rearrange("p (b e) -> p b e", b=G)
                    link(dve.tensor_reduce(g_max[0:T, :], sc, AX.X, ALU.max))
                    dve.tensor_tensor(v3(g_d), sc, per_tok(g_max), ALU.subtract).then_inc(gd_done.sem, 1)

                def gate():
                    dve.wait_ge(ge_done.sem, ge_done.at(q, 1))
                    link(dve.tensor_reduce(g_sum[0:T, :], v3(g_e), AX.X, ALU.add))
                    link(dve.reciprocal(g_rec[0:T, :], g_sum[0:T, :]))
                    link(dve.tensor_tensor(v3(g_p), v3(g_e), per_tok(g_rec), ALU.mult))
                    p_j = g_p[0:T, :].rearrange("p (b o j) -> p b o j", b=G, o=1).to_broadcast([T, G, E, E])
                    p_e = g_p[0:T, :].rearrange("p (b e o) -> p b e o", b=G, o=1).to_broadcast([T, G, E, E])
                    lower = tri[0:T, :].rearrange("p (o e j) -> p o e j", o=1, e=E).to_broadcast([T, G, E, E])
                    dve.tensor_tensor(v4(g_gt), p_j, p_e, ALU.is_gt)
                    link(dve.tensor_tensor(v4(g_ge), p_j, p_e, ALU.is_equal))
                    link(dve.tensor_tensor(v4(g_ge), v4(g_ge), lower, ALU.mult))
                    link(dve.tensor_tensor(v4(g_gt), v4(g_gt), v4(g_ge), ALU.add))
                    link(dve.tensor_reduce(v3(g_rank), v4(g_gt), AX.X, ALU.add))
                    link(dve.tensor_scalar(g_mask[0:T, :], g_rank[0:T, :], 1.5, None, ALU.is_lt))
                    link(dve.tensor_tensor(g_mask[0:T, :], g_mask[0:T, :], g_p[0:T, :], ALU.mult))
                    link(dve.tensor_reduce(g_sum[0:T, :], v3(g_mask), AX.X, ALU.add))
                    link(dve.tensor_scalar(g_sum[0:T, :], g_sum[0:T, :], 1e-9, None, ALU.add))
                    link(dve.reciprocal(g_rec[0:T, :], g_sum[0:T, :]))
                    dve.tensor_tensor(v3(gated), v3(g_mask), per_tok(g_rec), ALU.mult).then_inc(gated_done.sem, 1)
                    assert count[0] == gchain.n

                def first_norm(e):
                    dve.wait_ge(wo_done.sem, wo_done.at(q, e + 2))
                    dve.wait_ge(xbo_done.sem, xbo_done.at(q, e + 1))
                    dve.tensor_tensor(s_tok[0:T, :], psum[0:T, 6, :], xbo[0:T, :], ALU.add).then_inc(res_done.sem, 1)
                    dve.wait_ge(res_done.sem, res_done.at(q, e + 1))
                    norm_stats(q, e + 1, [tok(s_tok, b) for b in range(G)], tiles, (stats_done, aggr_done, veps_done, rstd_done))

                def first_norm_out(e):
                    dve.wait_ge(rstd_done.sem, rstd_done.at(q, e + 1))
                    dve.wait_ge(zsT_done.sem, zsT_done.at(q, e))
                    standardize([(tok(z_tok, b), tok(s_tok, b)) for b in range(G)], mv, rstd).then_inc(zs_done.sem, 1)

                def more(e, b):
                    if ahead and (e, b) == (4, 0):
                        a_norm1_out(n)
                    if b < 2 and (e + 2 < E or ahead and e + 2 == E):
                        rest(*((q, e + 3) if e + 2 < E else (n, 0)), b, 4 + b)
                    if ahead and (e, b) == (6, 0):
                        a_r_rest(n)
                    if (e, b) == (0, 1):
                        gate_scores()
                    if (e, b) == (0, 2):
                        gate()
                    if (e, b) == (1, 0):
                        dve.wait_ge(be2_done.sem, be2_done.at(q, 1))
                        dve.wait_ge(out_sent.sem, out_sent.at(q, 0))
                        dve.tensor_tensor(acc[0:T, :], psum[0:T, 6, :], h1_tok[0:T, :], ALU.add).then_inc(acc_init.sem, 1)
                    if e and b == 1:
                        first_norm(e - 1)
                    if e and b == 2:
                        first_norm_out(e - 1)
                    if ahead and e < E:
                        stage = {(0, 3): a_hbn, (1, 3): a_norm0, (2, 0): a_norm0_out, (3, 3): a_norm1,
                                 (5, 3): a_rotate}.get((e, b))
                        if stage:
                            stage(n)

                row_max(*steps[0])
                for i, (qq, unit, b, step) in enumerate(steps):
                    if i > 1:
                        norm_ctx(*steps[i - 2])
                    if i + 1 < len(steps):
                        row_max(*steps[i + 1])
                    if i:
                        spread_sums(*steps[i - 1])
                    more(unit - 1 if unit else E, b)
                norm_ctx(*steps[-2])
                spread_sums(*steps[-1])
                norm_ctx(*steps[-1])
                if not ahead:
                    first_norm(E - 1)
                    first_norm_out(E - 1)

                def second_norm(e):
                    i = 7 - e % 2
                    dve.wait_ge(yT_done.sem, yT_done.at(q, e + 1))
                    norm_stats(q, e + 1, [bank_tok(i, b) for b in range(G)], tiles,
                               (stats2_done, aggr2_done, veps2_done, rstd2_done))
                    g2 = wslice("g2_rows", e)[0:T]
                    dve.wait_ge(acc_done.sem, acc_done.at(q, e))
                    for b in range(G):
                        ins = dve.scalar_tensor_tensor(tok(w_tok, b), bank_tok(i, b), mv[0:T, 2 * b:2 * b + 1], g2,
                                                       ALU.subtract, ALU.mult)
                    ins.then_inc(w_done.sem, 1)
                    dve.wait_ge(rstd2_done.sem, rstd2_done.at(q, e + 1))
                    dve.tensor_tensor(rg[0:T, :], rstd[0:T, :], v3(gated)[:, :, e], ALU.mult).then_inc(rg_done.sem, 1)
                    dve.wait_ge(rg_done.sem, rg_done.at(q, e + 1))
                    for b in range(G):
                        ins = dve.scalar_tensor_tensor(tok(acc, b), tok(w_tok, b), rg[0:T, b:b + 1], tok(acc, b),
                                                       ALU.mult, ALU.add)
                    ins.then_inc(acc_done.sem, 1)

                for e in range(E):
                    if ahead and e == 1:
                        a_norm2(n, 7)
                    if ahead and e > 3:
                        rest(n, *((1, 0), (1, 1), (2, 0), (2, 1))[e - 4], 6 + e % 2)
                    dve.wait_ge(gelu2_done.sem, gelu2_done.at(q, e + 1))
                    if e:
                        dve.wait_ge(yT_done.sem, yT_done.at(q, e - 1))
                    dve.tensor_tensor(yT[e % 2][:, :], y2[:, :], x1T[:, e * C:(e + 1) * C], ALU.add).then_inc(y_done.sem, 1)
                    if ahead and e == 1:
                        a_norm2_out(n)
                    if e:
                        second_norm(e - 1)
                second_norm(E - 1)

            all_turns(dve, first, turn)

        @block.gpsimd
        def _(pool):
            for signal in Signal.all:
                pool.nop(nofuse=True).then_inc(signal.sem, signal.n)
            pool.wait_ge(zeroed, 1)
            pool.wait_ge(setup_dve, 3)
            pool.tensor_tensor(bn[:, 3:4], bn[:, 2:3], minus_half[:, 0:1], ALU.pow).then_inc(setup_rs, 1)

            def power(q, k, m, src, dst, veps_sig, rstd_sig):
                pool.wait_ge(veps_sig.sem, veps_sig.at(q, k))
                pool.tensor_tensor(dst[0:T, 0:m], src[0:T, 0:m], minus_half[0:T, 0:m], ALU.pow).then_inc(rstd_sig.sem, 1)

            def ahead_power(n, k):
                power(n, k + 1, (G, 2 * G, G)[k], a_veps, a_rstd, a_veps_done, a_rstd_done)

            def low(q, unit, side):
                mid_, done, parts, left = ((q_mid, q_low, q_part, q_left), (k_mid, k_low, k_part, k_left))[side]
                pool.wait_ge(mid_.sem, mid_.at(q, unit + 1))
                par = parity(unit)
                pool.tensor_tensor(parts[par][2][:, :], left[:, :], parts[par][1][:, :], ALU.subtract).then_inc(done.sem, 1)

            def r_lows(n):
                pool.wait_ge(r_mid.sem, r_mid.at(n, 1))
                pool.tensor_tensor(r_part[2][0:2 * HP, :], rotary_left[0:2 * HP, :], r_part[1][0:2 * HP, :],
                                   ALU.subtract).then_inc(r_low.sem, 1)

            def first():
                for k in range(2):
                    ahead_power(0, k)
                r_lows(0)
                low(0, 0, 0)
                low(0, 0, 1)
                ahead_power(0, 2)
                for unit in (1, 2):
                    for side in range(2):
                        low(0, unit, side)

            def turn(q, ahead):
                n = q + 1
                for e in range(E):
                    if ahead and e == 6:
                        r_lows(n)
                    after = (q, e + 3) if e + 2 < E else (n, 0)
                    if e + 2 < E or ahead and e + 2 == E:
                        low(*after, 0)
                    if e > 0:
                        power(q, e, G, veps, rstd, veps_done, rstd_done)
                    if e + 2 < E or ahead and e + 2 == E:
                        low(*after, 1)
                    if e == 0:
                        pool.wait_ge(z1_done.sem, z1_done.at(q, 1))
                    pool.wait_ge(res_done.sem, res_done.at(q, e))
                    for b in range(G):
                        ins = pool.tensor_tensor(tok(xbo, b), tok(x_tok, b), wslice("bo_rows", e)[0:T], ALU.add)
                    ins.then_inc(xbo_done.sem, 1)
                    if ahead and e == 1:
                        ahead_power(n, 0)
                    if ahead and e == 3:
                        ahead_power(n, 1)
                power(q, E, G, veps, rstd, veps_done, rstd_done)
                if ahead:
                    ahead_power(n, 2)
                for e in range(E):
                    power(q, e + 1, G, veps, rstd, veps2_done, rstd2_done)
                    if ahead and e > 3:
                        low(n, *((1, 0), (1, 1), (2, 0), (2, 1))[e - 4])

            all_turns(pool, first, turn)


def layouts(x, n):
    f = np.float32

    def rows(*parts, cols):
        out = np.zeros((128, cols), f)
        at = 0
        for p in parts:
            out[:p.shape[0], at:at + p.shape[1]] = p
            at += p.shape[1]
        return out

    def pad_heads(w):
        w = w.reshape(2, HG, DH, -1)
        out = np.zeros((2, HG, HP, w.shape[-1]), f)
        out[:, :, :DH] = w
        return out.reshape(2, HG * HP, -1).transpose(1, 0, 2).reshape(HG * HP, -1)

    by_dim = np.arange(D).reshape(H, DH).T.ravel()
    by_dim_r = np.arange(ROPE).reshape(H, DR).T.ravel()

    def rotary_cols(w):
        return [np.pad(w[:, i], ((0, 0), (0, HP - ROPE))) for i in (by_dim_r, by_dim_r ^ 1)]

    cut = SHIFTS[0] * D_IN
    wt = n["L0_tok_W"].T
    qkv = n["L0_ffn_Wqkv"].transpose(2, 0, 1).reshape(D, E, 3, D)
    bqkv = n["L0_ffn_bqkv"].reshape(E, 3, D)
    ukv = n["L0_attn_W_ukv"]
    bv = np.stack([pad_heads(bqkv[e, 2][:, None]) for e in range(E)])
    bf1 = n["L0_ffn_bf1"].reshape(E, FC, D)
    t = np.arange(T, dtype=f)
    sign = np.where(by_dim_r % 2 == 0, -1, 1).astype(f)[:, None]
    cos, sin = np.tile(np.cos(t), G)[None], np.tile(np.sin(t), G)[None]
    rope = np.concatenate([np.broadcast_to(cos, (ROPE, C)), sign * sin], 1)
    mask = np.where(np.arange(T)[None] <= np.arange(T)[:, None], 0, MASKED).astype(f)
    c = {
        "conv_w": rows(wt[:cut], wt[cut:], cols=2 * D),
        "wq": qkv[:, :, 0][:, :, by_dim].reshape(D, -1), "wk": qkv[:, :, 1][:, :, by_dim].reshape(D, -1), "wv": qkv[:, :, 2].reshape(D, -1),
        "wo": np.concatenate([pad_heads(w.T) for w in n["L0_ffn_Wo"]], 1),
        "w1": n["L0_ffn_W1"].transpose(2, 0, 1).reshape(D, -1),
        "w2": n["L0_ffn_W2"].reshape(E, D, FC, D).transpose(3, 0, 2, 1).reshape(D, -1),
        "mla_cat": np.concatenate([n["L0_attn_W_dq"], n["L0_attn_W_dkv"]], 1),
        "mla_uq": rows(n["L0_attn_W_uq"][:, by_dim], cols=D),
        "mla_uk": rows(ukv[:, :D][:, by_dim], cols=D), "mla_uv": rows(ukv[:, D:], cols=D),
        "mla_rope": rows(*rotary_cols(n["L0_attn_W_qr"]), *rotary_cols(n["L0_attn_W_kr"]), cols=4 * HP),
        "mla_wo": pad_heads(n["L0_attn_W_o"].T),
        "gate_w": n["L0_ffn_gate_Wk"].T, "gate_q": n["L0_ffn_expert_queries"].T,
        "cols": rows(*[n[k][:, None] for k in ("L0_tok_b", "L0_tok_gamma", "L0_tok_beta", "L0_ffn_gate_bk", "L0_attn_q_ln_g",
                                               "L0_attn_q_ln_b", "L0_attn_kv_ln_g", "L0_attn_kv_ln_b")], np.zeros((D, 1), f), cols=len(COLS)),
        "ecols": np.stack([bqkv[:, 0][:, by_dim], bqkv[:, 1][:, by_dim], *(bf1[:, i] for i in range(FC)), n["L0_ffn_bf2"], n["L0_ffn_g1"],
                           n["L0_ffn_be1"], bv[:, :, 0], bv[:, :, 1]]).reshape(-1, D).T,
        "bo_rows": np.broadcast_to(n["L0_ffn_bo"].reshape(1, -1), (128, E * D)),
        "g2_rows": np.broadcast_to(n["L0_ffn_g2"].reshape(1, -1), (128, E * D)),
        "be2": rows(n["L0_ffn_be2"], cols=D),
        "ident": np.eye(D, dtype=f),
        "causal": np.concatenate(
            [np.pad(mask, ((0, 128 - T), (0, 0))), np.pad(mask.T, ((0, 128 - T), (0, 0)))], 1),
        "rope_tab": rows(np.concatenate([np.pad(rope, ((0, HP - ROPE), (0, 0)))] * 2), cols=2 * C),
        "tri": np.broadcast_to(np.tril(np.ones((E, E), f), -1).reshape(1, -1), (128, E * E)),
    }
    return x.transpose(2, 0, 1), c


def kernel(**inputs):
    import concourse.bacc as bacc
    from concourse.bass_utils import run_bass_kernel_spmd

    named = {k: np.asarray(v) for k, v in inputs.items()}
    xw, consts = layouts(named.pop("x"), named)
    arrays = {f"in_{k}": np.ascontiguousarray(v) for k, v in {**consts, "x": xw}.items()}
    nc = bacc.Bacc("TRN2", target_bir_lowering=False, num_devices=1)
    aps = {k: nc.dram_tensor(k, v.shape, mybir.dt.from_np(v.dtype), kind="ExternalInput").ap() for k, v in arrays.items()}
    out = nc.dram_tensor("out", (B, T, D), F32, kind="ExternalOutput").ap()
    build_program(nc, {k: aps[f"in_{k}"] for k in consts}, aps["in_x"], out)
    return run_bass_kernel_spmd(nc, [arrays], core_ids=[0]).results[0]["out"]
```
